# Optimizing a Trainium2 kernel written in Bass

```python
import numpy as np
import jax
import jax.numpy as jnp

def _softmax(x, axis=-1):
    return jax.nn.softmax(x, axis=axis)

def _gelu(x):
    return jax.nn.gelu(x, approximate=True)

def _silu(x):
    return jax.nn.silu(x)

def _sigmoid(x):
    return jax.nn.sigmoid(x)

def _layernorm(x, axis=-1, eps=1e-05):
    m = jnp.mean(x, axis=axis, keepdims=True)
    v = jnp.var(x, axis=axis, keepdims=True)
    return (x - m) / jnp.sqrt(v + eps)

def _scatter_add(tgt, idx, src, axis=0):
    return tgt.at[idx].add(src)

def _segment_sum(src, seg, n):
    return jax.ops.segment_sum(src, seg, n)
kernel_name = 'mk_adj_resnorm_d1_adj_r2_79a59b'

def setup_inputs(seed: int=0):
    np.random.seed(seed)
    _w = jnp.asarray

    def _rec_inputs():
        import jax
        import jax.numpy as jnp
        _gk = jax.random.key(seed)
        x = -0.0005963 + 1.001 * jax.random.normal(jax.random.fold_in(_gk, 1), (16, 512, 384), jnp.float32)
        _a = jax.random.bernoulli(jax.random.fold_in(_gk, 2), 0.03125, (16, 512, 512))
        _a = jnp.logical_or(_a, jnp.swapaxes(_a, -1, -2))
        _a = jnp.logical_or(_a, jnp.eye(512, dtype=bool))
        adj = _a
        return (x, adj)
    x, adj = _rec_inputs()

    def _L0_gnn_setup():
        import jax, jax.numpy as jnp
        import numpy as np
        ATT_HEAD = 12
        IN_DIM = 384
        OUT_DIM = IN_DIM // ATT_HEAD
        LEAKY_ALPHA = 0.2
        B, N = (8, 256)
        key = jax.random.key(seed)
        ks = jax.random.split(key, 8)
        feat_in = jax.random.normal(ks[0], (B, N, IN_DIM), dtype=jnp.float32)
        adj = jax.random.randint(ks[1], (B, N, N), 0, 2) > 0
        lim_W = float(np.sqrt(6.0 / (IN_DIM + OUT_DIM)))
        W = jax.random.uniform(ks[2], (ATT_HEAD, IN_DIM, OUT_DIM), minval=-lim_W, maxval=lim_W, dtype=jnp.float32)
        b = jnp.zeros((OUT_DIM,), dtype=jnp.float32)
        lim_w = float(np.sqrt(6.0 / (OUT_DIM + 1)))
        w_src = jax.random.uniform(ks[3], (ATT_HEAD, OUT_DIM, 1), minval=-lim_w, maxval=lim_w, dtype=jnp.float32)
        w_dst = jax.random.uniform(ks[4], (ATT_HEAD, OUT_DIM, 1), minval=-lim_w, maxval=lim_w, dtype=jnp.float32)
        std_H = float(np.sqrt(2.0 / (IN_DIM + IN_DIM)))
        H_w = jax.random.normal(ks[5], (IN_DIM, IN_DIM), dtype=jnp.float32) * std_H
        H_b = jax.random.normal(ks[6], (IN_DIM,), dtype=jnp.float32) * 0.01
        return {'feat_in': feat_in, 'adj': adj, 'W': W, 'b': b, 'w_src': w_src, 'w_dst': w_dst, 'H_w': H_w, 'H_b': H_b}
    _L0_gnn_all = _L0_gnn_setup()
    _L0_gnn_in = {k: v for k, v in _L0_gnn_all.items() if k in ('W', 'b', 'w_src', 'w_dst', 'H_w', 'H_b')}
    del _L0_gnn_all
    return {'x': x, 'adj': adj, 'L0_gnn_W': _L0_gnn_in['W'], 'L0_gnn_b': _L0_gnn_in['b'], 'L0_gnn_w_src': _L0_gnn_in['w_src'], 'L0_gnn_w_dst': _L0_gnn_in['w_dst'], 'L0_gnn_H_w': _L0_gnn_in['H_w'], 'L0_gnn_H_b': _L0_gnn_in['H_b']}

def reference(x, adj, L0_gnn_W, L0_gnn_b, L0_gnn_w_src, L0_gnn_w_dst, L0_gnn_H_w, L0_gnn_H_b):
    import jax
    import jax.numpy as jnp

    def _L0_gnn_ref(feat_in, adj, W, b, w_src, w_dst, H_w, H_b):
        import jax, jax.numpy as jnp
        import numpy as np
        ATT_HEAD = 12
        IN_DIM = 384
        OUT_DIM = IN_DIM // ATT_HEAD
        LEAKY_ALPHA = 0.2
        B, N = (8, 256)
        h = jnp.einsum('bnd,ade->bane', feat_in, W)
        th = jnp.tanh(h)
        attn_src = jnp.einsum('bane,aeo->bano', th, w_src)
        attn_dst = jnp.einsum('bane,aeo->bano', th, w_dst)
        attn = attn_src + jnp.swapaxes(attn_dst, 2, 3)
        attn = jnp.where(attn >= 0, attn, LEAKY_ALPHA * attn)
        mask = ~adj[:, None, :, :]
        attn = jnp.where(mask, jnp.float32(-999.0), attn)
        attn = jax.nn.softmax(attn, axis=-1)
        feat_out = jnp.einsum('banm,bame->bane', attn, h) + b
        feat_out = jnp.swapaxes(feat_out, 1, 2).reshape(feat_in.shape[0], feat_in.shape[1], -1)
        feat_out = jax.nn.elu(feat_out)
        gate = jax.nn.sigmoid(feat_in @ H_w.T + H_b)
        return gate * feat_out + (1.0 - gate) * feat_in
    x = _layernorm(x + _L0_gnn_ref(x, adj, L0_gnn_W, L0_gnn_b, L0_gnn_w_src, L0_gnn_w_dst, L0_gnn_H_w, L0_gnn_H_b), axis=-1)
    return x

_drawn_inputs = setup_inputs


def setup_inputs(seed=0):
    import zlib

    import numpy as np

    out = dict(_drawn_inputs(seed))
    spreads = {'L0_gnn_b': (0.0, 0.1)}
    factors = {'L0_gnn_H_b': 35.675}
    for name, (base, spread) in spreads.items():
        noise = np.random.default_rng([zlib.crc32(name.encode()), seed]).standard_normal(out[name].shape)
        drawn = base * np.exp(spread * noise) if base else spread * noise
        out[name] = jnp.asarray(drawn.astype(out[name].dtype))
    for name, factor in factors.items():
        out[name] = (out[name] * factor).astype(out[name].dtype)
    return out
```

```python
import concourse.bass as bass
from concourse import mybir
from contextlib import ExitStack

F32 = mybir.dt.float32
F32R = mybir.dt.float32r
BF16 = mybir.dt.bfloat16
U8 = mybir.dt.uint8
ALU = mybir.AluOpType
ACT = mybir.ActivationFunctionType
AX = mybir.AxisListType
RMAX = bass.bass_isa.ReduceOp.max

P = 128
ALPHA = 0.2
EPS = 1e-5


def gat_layernorm(nc, x, xT, adjT, W, HwT, w_src, w_dst, bias, H_b, out):
    B, N, D = x.shape
    H, E = w_src.shape
    C = N // P
    KD = D // P
    HP = H // 2
    VW = 64
    SLOTS = 16
    NPART = 3
    assert N == 512 and H * E == D and B % 2 == 0

    ctx = ExitStack()
    with ctx:
        def sb(name, shape, dt=F32):
            return ctx.enter_context(nc.sbuf_tensor(name, shape, dt))

        def pb(name):
            return ctx.enter_context(nc.psum_tensor(name, [P, 512], F32))

        def sem(name):
            return ctx.enter_context(nc.semaphore(name))

        xT_in = sb("xT_in", [P, KD, N])
        xT_hi = sb("xT_hi", [P, KD, N], F32R)
        xT_lo = sb("xT_lo", [P, KD, N], F32R)
        x_in = sb("x_in", [P, 2, C, D])
        adj_in = sb("adj_in", [P, 2, C, N], U8)
        w_hi = sb("w_hi", [P, KD, 2 * D], F32R)
        w_lo = sb("w_lo", [P, KD, 2 * D], F32R)
        src_row = sb("src_row", [P, D])
        dst_row = sb("dst_row", [P, D])
        bias_row = sb("bias_row", [P, H, E])
        gate_bias_in = sb("gate_bias_in", [P, D])
        gate_bias = sb("gate_bias", [P, D], F32R)
        gate_bias_sel = sb("gate_bias_sel", [P, P], F32R)
        ident = sb("ident", [P, P])
        ident_bf = sb("ident_bf", [P, P], BF16)
        head_sel = sb("head_sel", [P, H, P], BF16)
        mean_w = sb("mean_w", [P, P])
        half = sb("half", [P, C])
        minus1 = sb("minus1", [P, 1])
        h_sb = sb("h_sb", [P, C, D])
        hb = sb("hb", [P, C, D])
        hb_sum = sb("hb_sum", [P, 2, D])
        th = sb("th", [P, C, D])
        prod = sb("prod", [P, 2, C, D])
        sd = sb("sd", [P, 2, C, H])
        d_max_c = sb("d_max_c", [P, H])
        d_max = sb("d_max", [P, H])
        d_rel = sb("d_rel", [P, C, H])
        s_rel = sb("s_rel", [P, C, H])
        s_exp = sb("s_exp", [P, C, H])
        v = sb("v", [P, C, H])
        v_rest = sb("v_rest", [P, C, H])
        v_parts = sb("v_parts", [P, C, P], BF16)
        v_T = sb("v_T", [P, 2, N], BF16)
        u = sb("u", [P, 2, C, H])
        vals = sb("vals", [P, 2, C, H, VW])
        hb_mean = sb("hb_mean", [P, 2, D])
        gate = sb("gate", [P, 2, C, D])
        ew = sb("ew", [P, SLOTS, N])
        att_T = sb("att_T", [P, 2, N])
        den = sb("den", [P, C, 2])
        rden = sb("rden", [P, C, 2])
        alone = sb("alone", [P, 2, C])
        att = sb("att", [P, 2, C, D])
        ex = sb("ex", [P, C, D])
        y = sb("y", [P, C, D])
        stats = sb("stats", [P, C, 6])
        mv = sb("mv", [P, C, 2])
        var = sb("var", [P, C])
        rstd = sb("rstd", [P, C])
        shift = sb("shift", [P, C])
        y_out = sb("y_out", [P, C, D])
        w_in = ew[:, 0:5, :].rearrange("p s n -> p (s n)")[:, 0:2 * KD * D].rearrange("p (k n) -> p k n", k=KD)

        HG = [pb("hg0"), pb("hg1")]
        VB = [pb("vb0"), pb("vb1")]
        OUT = pb("out_T")
        TR = [pb("tr0"), pb("tr1")]
        VTP = pb("v_T_ps")
        vtp = VTP[:, 0:256].bitcast(BF16)

        names = """ld_w ld_rows ld_xT ld_x0 ld_x1 ld_adj0 ld_adj1 st_y
            consts pool_setup dve_setup act_setup
            xhi_done xlo_done h_done th_done hcopy_done g_done gate_done hb_done hb_sum_done hm_done hm_copied
            prod_done scores d_max_done exps_done vtp_done vT_done vals_done
            vb_ready ew_ready ew_free out_done outT_copied tr_done den_done att_done
            alone_done att1_done elu_exp_done epi rstd_done y_done""".split()
        S = {n: sem(n) for n in names}
        ld_x, ld_adj = [S["ld_x0"], S["ld_x1"]], [S["ld_adj0"], S["ld_adj1"]]
        NSC = 9
        NEP = 4 + 2 * C + 2

        x_v = x.rearrange("b (c p) d -> b p c d", p=P)
        xT_v = xT.rearrange("b (k p) n -> b p k n", p=P)
        adj_v = adjT.rearrange("b (c p) n -> b p c n", p=P)
        out_v = out.rearrange("b (c p) d -> b p c d", p=P)

        block = ctx.enter_context(nc.Block())

        def program(eng, step, before=None, after=None):
            if before:
                before()
            step(0, 0, True, False)
            with eng.Fori(0, (B - 2) // 2) as i:
                step(2 * i + 1, 1, False, False)
                step(2 * i + 2, 0, False, False)
            step(B - 1, (B - 1) % 2, False, True)
            if after:
                after()

        @block.sync
        def _(sp):
            def before():
                sp.sem_inc(S["st_y"], 16)
                sp.dma_start(w_in[:, :, 0:D], W.rearrange("(k p) n -> p k n", p=P)).then_inc(S["ld_w"], 16)
                sp.dma_start(w_in[:, :, D:2 * D], HwT.rearrange("(k p) n -> p k n", p=P)).then_inc(S["ld_w"], 16)
                sp.dma_start(xT_in[:], xT_v[0]).then_inc(S["ld_xT"], 16)
                row = lambda a: a.rearrange("h e -> (h e)").rearrange("(o n) -> o n", o=1).broadcast_to([P, D])
                sp.dma_start(src_row[:], row(w_src)).then_inc(S["ld_rows"], 16)
                sp.dma_start(dst_row[:], row(w_dst)).then_inc(S["ld_rows"], 16)
                for hh in range(H):
                    sp.dma_start(bias_row[:, hh, :], bias.rearrange("(o n) -> o n", o=1).broadcast_to([P, E])).then_inc(S["ld_rows"], 16)
                sp.wait_ge(S["pool_setup"], 1)
                for r in (0, 32):
                    sp.dma_start(gate_bias_in[r:r + 1, :], H_b.rearrange("(o n) -> o n", o=1)).then_inc(S["ld_rows"], 16)
                sp.dma_start(adj_in[:, 0], adj_v[0]).then_inc(ld_adj[0], 16)

            def step(b, q, first, last):
                if not last:
                    sp.wait_ge(S["xhi_done"], b + 1)
                    sp.wait_ge(S["xlo_done"], b + 1)
                    sp.dma_start(xT_in[:], xT_v[b + 1]).then_inc(S["ld_xT"], 16)
                if not first:
                    sp.wait_ge(S["alone_done"], b + 1)
                sp.dma_start(x_in[:, q], x_v[b]).then_inc(ld_x[q], 16)
                if not last:
                    sp.dma_start(adj_in[:, 1 - q], adj_v[b + 1]).then_inc(ld_adj[1 - q], 16)
                if not first:
                    store(b - 1)

            def store(b):
                sp.wait_ge(S["y_done"], C * b + 2 * C)
                sp.dma_start(out_v[b], y_out[:]).then_inc(S["st_y"], 16)

            def after():
                store(B - 1)
                sp.wait_ge(S["st_y"], 16 * B + 16)

            program(sp, step, before, after)

        @block.gpsimd
        def _(pool):
            g = nc.gpsimd

            def before():
                g.memset(gate_bias_in[:], 0.0).then_inc(S["pool_setup"], 1)
                g.memset(ident[:], 0.0).then_inc(S["pool_setup"], 1)
                g.memset(ident_bf[:], 0.0).then_inc(S["pool_setup"], 1)
                g.memset(head_sel[:], 0.0).then_inc(S["pool_setup"], 1)
                g.memset(mean_w[:], 1.0 / N).then_inc(S["pool_setup"], 1)
                g.memset(half[:], -0.5).then_inc(S["pool_setup"], 1)
                g.memset(minus1[:], -1.0).then_inc(S["pool_setup"], 1)
                pool.wait_ge(S["pool_setup"], 7)
                for m in (ident, ident_bf):
                    g.affine_select(out=m[:], in_=m[:], compare_op=ALU.not_equal, fill=1.0, base=0,
                                    pattern=[[-1, P]], channel_multiplier=1).then_inc(S["pool_setup"], 1)
                for k in range(NPART):
                    g.affine_select(out=head_sel[:], in_=head_sel[:], compare_op=ALU.not_equal, fill=1.0,
                                    base=-H * k, pattern=[[-1, H], [0, P]],
                                    channel_multiplier=1).then_inc(S["pool_setup"], 1)
                    pool.wait_ge(S["pool_setup"], 10 + k)
                pool.wait_ge(S["ld_w"], 32)
                pool.wait_ge(S["act_setup"], 1)
                g.tensor_tensor(w_lo[:], w_in, w_hi[:].bitcast(F32), ALU.subtract).then_inc(S["pool_setup"], 1)
                pool.wait_ge(S["ld_rows"], 16 * (4 + H))
                g.tensor_scalar(bias_row[:], bias_row[:], 1.0, 1.0, ALU.mult, ALU.add).then_inc(S["pool_setup"], 1)
                pool.wait_ge(S["pool_setup"], 14)
                prepare(0, 0)

            def prepare(b, q):
                pool.wait_ge(S["xhi_done"], b + 1)
                pool.wait_ge(S["g_done"], C * b)
                g.tensor_tensor(xT_lo[:], xT_in[:], xT_hi[:].bitcast(F32), ALU.subtract).then_inc(S["xlo_done"], 1)
                for c in range(C):
                    pool.wait_ge(S["th_done"], C * b + c + 1)
                    for k, row in ((0, src_row), (1, dst_row)):
                        g.tensor_tensor(prod[:, k, c], th[:, c], row[:], ALU.mult).then_inc(S["prod_done"], 1)
                pool.wait_ge(S["hcopy_done"], C * b + C)
                pool.wait_ge(S["vals_done"], C * b)
                g.tensor_tensor(hb[:], h_sb[:], bias_row[:].rearrange("p h e -> p (h e)").unsqueeze(1).broadcast_to([P, C, D]),
                                ALU.add).then_inc(S["hb_done"], 1)
                pool.wait_ge(S["hb_done"], b + 1)
                pool.wait_ge(S["hm_done"], b)
                pool.wait_ge(S["scores"], NSC * b + 2)
                g.tensor_tensor(hb_sum[:], hb[:, 0:2], hb[:, 2:4], ALU.add).then_inc(S["hb_sum_done"], 1)
                g.partition_all_reduce(d_max[:], d_max_c[:], P, RMAX).then_inc(S["d_max_done"], 1)
                pool.wait_ge(S["exps_done"], 3 * b + 2)
                for c in range(C):
                    o = vals[:, q, c]
                    g.tensor_tensor(o[:, :, 0:E], hb[:, c].rearrange("p (h e) -> p h e", e=E),
                                    o[:, :, E:E + 1].broadcast_to([P, H, E]), ALU.mult).then_inc(S["vals_done"], 1)

            def finish(b):
                pool.wait_ge(S["epi"], NEP * b + NEP - 1)
                g.tensor_tensor(rstd[:], var[:], half[:], ALU.pow).then_inc(S["rstd_done"], 1)

            def step(b, q, first, last):
                if not last:
                    prepare(b + 1, 1 - q)
                if not first:
                    finish(b - 1)

            program(pool, step, before, lambda: finish(B - 1))

        @block.scalar
        def _(act):
            a = nc.scalar

            def before():
                a.sem_inc(S["y_done"], C)
                act.wait_ge(S["ld_w"], 32)
                a.activation(w_hi[:], w_in, ACT.Copy).then_inc(S["act_setup"], 1)
                split(0)
                for c in range(C):
                    features(0, c)
                for c in range(C):
                    gates(0, 0, c, True)
                act.wait_ge(S["pool_setup"], 14)
                exps(0, 0)
                copy_mean(0, 0)
                copy_vT(0, 0)

            def split(b):
                act.wait_ge(S["ld_xT"], 16 * b + 16)
                act.wait_ge(S["g_done"], C * b)
                a.activation(xT_hi[:], xT_in[:], ACT.Copy).then_inc(S["xhi_done"], 1)

            def features(b, c):
                act.wait_ge(S["h_done"], C * b + c + 1)
                act.wait_ge(S["prod_done"], 2 * C * b)
                a.activation(th[:, c], HG[c % 2][:, 0:D], ACT.Tanh).then_inc(S["th_done"], 1)
                act.wait_ge(S["hb_done"], b)
                a.activation(h_sb[:, c], HG[c % 2][:, 0:D], ACT.Copy).then_inc(S["hcopy_done"], 1)

            def gates(b, q, c, first):
                act.wait_ge(S["g_done"], C * b + c + 1)
                if not first:
                    act.wait_ge(S["epi"], NEP * (b - 2) + 3)
                a.activation(gate[:, q, c], HG[c % 2][:, 0:D], ACT.Tanh, scale=0.5).then_inc(S["gate_done"], 1)

            def exps(b, q):
                act.wait_ge(S["scores"], NSC * b + 3)
                a.activation(vals[:, q, :, :, E], d_rel[:], ACT.Exp, scale=ALPHA).then_inc(S["exps_done"], 1)
                a.activation(u[:, q], d_rel[:], ACT.Exp, scale=1 - ALPHA).then_inc(S["exps_done"], 1)
                act.wait_ge(S["scores"], NSC * b + 5)
                a.activation(v[:], s_exp[:], ACT.Exp).then_inc(S["exps_done"], 1)

            def copy_mean(b, q):
                act.wait_ge(S["hm_done"], b + 1)
                a.activation(hb_mean[:, q], HG[0][:, 0:D], ACT.Copy).then_inc(S["hm_copied"], 1)

            def copy_vT(b, q):
                act.wait_ge(S["vtp_done"], b + 1)
                a.activation(v_T[:, q], vtp, ACT.Copy).then_inc(S["vT_done"], 1)

            def copy_out(b, j):
                act.wait_ge(S["out_done"], HP * b + j + 1)
                if j < 2:
                    act.wait_ge(S["tr_done"], HP * b + 0)
                else:
                    act.wait_ge(S["tr_done"], HP * b + j - 1)
                a.activation(att_T[:, j % 2], OUT[:], ACT.Copy).then_inc(S["outT_copied"], 1)

            def elu_exp(b, q):
                act.wait_ge(S["att1_done"], C * b + C)
                a.activation(ex[:], att[:, q], ACT.Exp, bias=minus1[:, 0:1]).then_inc(S["elu_exp_done"], 1)

            def normalise(b):
                act.wait_ge(S["epi"], NEP * b + NEP)
                act.wait_ge(S["st_y"], 16 * b + 16)
                for c in range(C):
                    a.activation(y_out[:, c], y[:, c], ACT.Identity, bias=shift[:, c:c + 1],
                                 scale=rstd[:, c:c + 1]).then_inc(S["y_done"], 1)

            def step(b, q, first, last):
                if not last:
                    split(b + 1)
                copy_out(b, 0)
                if not first:
                    elu_exp(b - 1, 1 - q)
                if not last:
                    features(b + 1, 0)
                    features(b + 1, 1)
                copy_out(b, 1)
                if not last:
                    features(b + 1, 2)
                    features(b + 1, 3)
                copy_out(b, 2)
                if not last:
                    gates(b + 1, 1 - q, 0, first)
                    gates(b + 1, 1 - q, 1, first)
                copy_out(b, 3)
                if not last:
                    gates(b + 1, 1 - q, 2, first)
                    gates(b + 1, 1 - q, 3, first)
                    exps(b + 1, 1 - q)
                copy_out(b, 4)
                if not last:
                    copy_mean(b + 1, 1 - q)
                    copy_vT(b + 1, 1 - q)
                copy_out(b, 5)
                if not first:
                    normalise(b - 1)

            def after():
                elu_exp(B - 1, (B - 1) % 2)
                normalise(B - 1)

            program(act, step, before, after)

        @block.vector
        def _(dve):
            ve = nc.vector

            def before():
                ve.memset(vals[:, :, :, :, :], 0.0).then_inc(S["dve_setup"], 1)
                ve.memset(v_parts[:], 0.0).then_inc(S["dve_setup"], 1)
                ve.memset(gate_bias_sel[:].bitcast(F32), 0.0).then_inc(S["dve_setup"], 1)
                dve.wait_ge(S["dve_setup"], 3)
                for r in (0, 32):
                    ve.memset(gate_bias_sel[r:r + 1, :].bitcast(F32), 1.0).then_inc(S["dve_setup"], 1)
                dve.wait_ge(S["ld_rows"], 16 * (4 + H))
                ve.tensor_copy(gate_bias[:], gate_bias_in[:]).then_inc(S["dve_setup"], 1)
                dve.wait_ge(S["dve_setup"], 6)
                ve.tensor_tensor(gate_bias[32:33, :], gate_bias_in[32:33, :], gate_bias[32:33, :].bitcast(F32),
                                 ALU.subtract).then_inc(S["dve_setup"], 1)
                dve.wait_ge(S["dve_setup"], 7)
                scores_sd(0)
                scores_rel(0)
                split_v(0)

            def sc(b, k):
                dve.wait_ge(S["scores"], NSC * b + k)

            def scores_sd(b):
                dve.wait_ge(S["prod_done"], 2 * C * (b + 1))
                ve.tensor_reduce(sd[:].rearrange("p k c h -> p (k c h)"), prod[:].rearrange("p k c (h e) -> p (k c h) e", e=E),
                                 AX.X, ALU.add).then_inc(S["scores"], 1)
                sc(b, 1)
                ve.tensor_reduce(d_max_c[:], sd[:, 1].rearrange("p c h -> p h c"), AX.X, ALU.max).then_inc(S["scores"], 1)

            def scores_rel(b):
                dve.wait_ge(S["d_max_done"], b + 1)
                m = d_max[:].unsqueeze(1).broadcast_to([P, C, H])
                ve.tensor_tensor(d_rel[:], sd[:, 1], m, ALU.subtract).then_inc(S["scores"], 1)
                ve.tensor_tensor(s_rel[:], sd[:, 0], m, ALU.add).then_inc(S["scores"], 1)
                sc(b, 4)
                ve.tensor_scalar(s_exp[:], s_rel[:], ALPHA - 1, 0.0, ALU.mult, ALU.min).then_inc(S["scores"], 1)

            def split_v(b):
                dve.wait_ge(S["exps_done"], 3 * b + 3)
                dve.wait_ge(S["vtp_done"], b)
                ve.tensor_copy(v_parts[:, :, 0:H], v[:]).then_inc(S["scores"], 1)
                sc(b, 6)
                ve.tensor_tensor(v_rest[:], v[:], v_parts[:, :, 0:H], ALU.subtract).then_inc(S["scores"], 1)
                sc(b, 7)
                ve.tensor_copy(v_parts[:, :, H:2 * H], v_rest[:]).then_inc(S["scores"], 1)
                sc(b, 8)
                ve.tensor_tensor(v_parts[:, :, 2 * H:3 * H], v_rest[:], v_parts[:, :, H:2 * H],
                                 ALU.subtract).then_inc(S["scores"], 1)

            def edges(b, q, h):
                dve.wait_ge(S["vb_ready"], H * b + h + 1)
                for c in range(C):
                    t = 8 * (h // 2) + 4 * (h % 2) + c
                    dve.wait_ge(S["ew_free"], 4 * H * b + 8 * (h // 2) + 2 * c + h % 2 + 1)
                    ve.scalar_tensor_tensor(out=ew[:, t % SLOTS, :], in0=VB[h % 2][:], scalar=u[:, q, c, h:h + 1],
                                            in1=adj_in[:, q, c, :], op0=ALU.max, op1=ALU.mult).then_inc(S["ew_ready"], 1)

            def attended(b, q, j):
                dve.wait_ge(S["tr_done"], HP * b + j + 1)
                t = TR[j % 2][:].rearrange("p (c k w) -> p c k w", c=C, k=2)
                if j == 0:
                    ve.tensor_scalar(alone[:, q], t[:, :, 0, E], 0.0, None, ALU.is_equal).then_inc(S["alone_done"], 1)
                dve.wait_ge(S["att_done"], HP * b + j)
                ve.tensor_scalar(rden[:], t[:, :, :, E], 0.0, None, ALU.is_equal).then_inc(S["den_done"], 1)
                dve.wait_ge(S["den_done"], 3 * (HP * b + j) + 1)
                ve.tensor_tensor(den[:], t[:, :, :, E], rden[:], ALU.add).then_inc(S["den_done"], 1)
                dve.wait_ge(S["den_done"], 3 * (HP * b + j) + 2)
                ve.reciprocal(rden[:], den[:]).then_inc(S["den_done"], 1)
                dve.wait_ge(S["den_done"], 3 * (HP * b + j) + 3)
                o = att[:, q].rearrange("p c (h e) -> p c h e", e=E)[:, :, 2 * j:2 * j + 2, :]
                ve.tensor_tensor(o, t[:, :, :, 0:E], rden[:].unsqueeze(3).broadcast_to([P, C, 2, E]),
                                 ALU.mult).then_inc(S["att_done"], 1)

            def add_means(b, q):
                dve.wait_ge(S["att_done"], HP * b + HP)
                dve.wait_ge(S["hm_copied"], b + 1)
                dve.wait_ge(S["alone_done"], b + 1)
                for c in range(C):
                    ve.scalar_tensor_tensor(out=att[:, q, c], in0=hb_mean[:, q], scalar=alone[:, q, c:c + 1],
                                            in1=att[:, q, c], op0=ALU.mult, op1=ALU.add).then_inc(S["att1_done"], 1)

            def ep(b, k):
                dve.wait_ge(S["epi"], NEP * b + k)

            def mix(b, q):
                dve.wait_ge(S["elu_exp_done"], b + 1)
                dve.wait_ge(S["att1_done"], C * b + C)
                ve.scalar_tensor_tensor(out=ex[:], in0=ex[:], scalar=1.0, in1=att[:, q], op0=ALU.min,
                                        op1=ALU.max).then_inc(S["epi"], 1)
                ep(b, 1)
                dve.wait_ge(ld_x[q], 8 * (b - q) + 16)
                ve.scalar_tensor_tensor(out=ex[:], in0=ex[:], scalar=-1.0, in1=x_in[:, q], op0=ALU.add,
                                        op1=ALU.subtract).then_inc(S["epi"], 1)
                ep(b, 2)
                dve.wait_ge(S["gate_done"], C * b + C)
                ve.scalar_tensor_tensor(out=ex[:], in0=gate[:, q], scalar=1.0, in1=ex[:], op0=ALU.add,
                                        op1=ALU.mult).then_inc(S["epi"], 1)
                ep(b, 3)
                dve.wait_ge(S["y_done"], C * b + C)
                ve.scalar_tensor_tensor(out=y[:], in0=x_in[:, q], scalar=4.0, in1=ex[:], op0=ALU.mult,
                                        op1=ALU.add).then_inc(S["epi"], 1)

            def moments(b):
                ep(b, 4)
                for c in range(C):
                    ve.bn_stats(stats[:, c], y[:, c]).then_inc(S["epi"], 1)

            def aggregate(b):
                for c in range(C):
                    ve.bn_aggr(mv[:, c], stats[:, c]).then_inc(S["epi"], 1)
                ep(b, 4 + 2 * C)
                ve.tensor_scalar(var[:], mv[:, :, 1], 4 * EPS, None, ALU.add).then_inc(S["epi"], 1)

            def moments2(b):
                dve.wait_ge(S["rstd_done"], b + 1)
                ve.scalar_tensor_tensor(out=shift[:], in0=mv[:, :, 0], scalar=-1.0, in1=rstd[:], op0=ALU.mult,
                                        op1=ALU.mult).then_inc(S["epi"], 1)

            def step(b, q, first, last):
                dve.wait_ge(ld_adj[q], 8 * (b - q) + 16)
                dve.wait_ge(S["exps_done"], 3 * b + 3)
                for j in range(HP):
                    edges(b, q, 2 * j)
                    if j:
                        attended(b, q, j - 1)
                    if j == 0 and not first:
                        add_means(b - 1, 1 - q)
                    if j == 1 and not first:
                        mix(b - 1, 1 - q)
                    if j == 4 and not last:
                        scores_rel(b + 1)
                    if j == 3 and not first:
                        ep(b - 1, 4 + C)
                    edges(b, q, 2 * j + 1)
                    if j == 2 and not first:
                        moments(b - 1)
                    if j == 3 and not first:
                        aggregate(b - 1)
                    if j == 3 and not last:
                        scores_sd(b + 1)
                    if j == 4 and not first:
                        moments2(b - 1)
                    if j == 4 and not last:
                        split_v(b + 1)
                attended(b, q, HP - 1)

            def after():
                q = (B - 1) % 2
                add_means(B - 1, q)
                mix(B - 1, q)
                moments(B - 1)
                ep(B - 1, 4 + C)
                aggregate(B - 1)
                moments2(B - 1)

            program(dve, step, before, after)

        @block.tensor
        def _(pe):
            te = nc.tensor

            def before():
                te.sem_inc(S["ew_free"], SLOTS)
                pe.wait_ge(S["pool_setup"], 14)
                pe.wait_ge(S["dve_setup"], 7)
                for c in range(C):
                    features(0, c)
                for c in range(C):
                    gates(0, c)
                means(0)
                transpose_v(0)
                broadcast_v(0, 0, 0)
                broadcast_v(0, 0, 1)

            def products(bank, c, col, extra):
                o = bank[:, 0:D]
                n = slice(c * P, (c + 1) * P)
                mms = []
                for k in range(KD):
                    mms += [(xT_hi[:, k, n], w_hi[:, k, col:col + D]), (xT_hi[:, k, n], w_lo[:, k, col:col + D])]
                for k in range(KD):
                    mms.append((xT_lo[:, k, n], w_hi[:, k, col:col + D]))
                mms += extra
                for i, (l, r) in enumerate(mms):
                    last = te.matmul(o, l, r, start=(i == 0), stop=(i == len(mms) - 1))
                return last

            def features(b, c):
                if c == 0:
                    pe.wait_ge(S["xhi_done"], b + 1)
                    pe.wait_ge(S["xlo_done"], b + 1)
                if c == 0:
                    pe.wait_ge(S["hm_copied"], b)
                elif c == 1:
                    pe.wait_ge(S["gate_done"], C * b)
                else:
                    pe.wait_ge(S["hcopy_done"], C * b + c - 1)
                products(HG[c % 2], c, 0, []).then_inc(S["h_done"], 1)

            def gates(b, c):
                if c < 2:
                    pe.wait_ge(S["hcopy_done"], C * b + c + 3)
                else:
                    pe.wait_ge(S["gate_done"], C * b + c - 1)
                products(HG[c % 2], c, D, [(gate_bias_sel[:], gate_bias[:])]).then_inc(S["g_done"], 1)

            def means(b):
                pe.wait_ge(S["hb_sum_done"], b + 1)
                pe.wait_ge(S["gate_done"], C * b + 3)
                for k in range(2):
                    last = te.matmul(HG[0][:, 0:D], mean_w[:], hb_sum[:, k], start=(k == 0), stop=(k == 1))
                last.then_inc(S["hm_done"], 1)

            def transpose_v(b):
                pe.wait_ge(S["scores"], NSC * b + NSC)
                pe.wait_ge(S["vT_done"], b)
                for c in range(C):
                    last = te.transpose(vtp[:, c * P:(c + 1) * P], v_parts[:, c], ident_bf[:])
                last.then_inc(S["vtp_done"], 1)

            def broadcast_v(b, q, h):
                if h == 0:
                    pe.wait_ge(S["vT_done"], b + 1)
                if h > 1 or not isinstance(b, int) or b:
                    pe.wait_ge(S["ew_ready"], 4 * H * b + 4 * (h - 1))
                te.matmul(VB[h % 2][:], head_sel[:, h], v_T[:, q], start=True, stop=True).then_inc(S["vb_ready"], 1)

            def broadcast_next(b, q, h, last):
                if h + 2 < H:
                    broadcast_v(b, q, h + 2)
                elif not last:
                    broadcast_v(b + 1, 1 - q, h + 2 - H)

            def attend(b, q, j, last):
                pe.wait_ge(S["outT_copied"], HP * b + j)
                if j == 0:
                    pe.wait_ge(S["vals_done"], C * b + C)
                for c in range(C):
                    for k in range(2):
                        h = 2 * j + k
                        t = 8 * j + 4 * k + c
                        pe.wait_ge(S["ew_ready"], 4 * H * b + t + 1)
                        if k == 1 and c == C - 1:
                            broadcast_next(b, q, h, last)
                        mm = te.matmul(OUT[VW * k:VW * k + VW, :], vals[:, q, c, h, :], ew[:, t % SLOTS, :],
                                         start=(c == 0), stop=(c == C - 1))
                        mm.then_inc(S["ew_free"], 1)
                        if k == 0 and c == 0:
                            broadcast_next(b, q, h, last)
                pe.wait_ge(S["ew_free"], SLOTS + 4 * H * b + 8 * j + 8)
                te.sem_inc(S["out_done"], 1)

            def transpose_out(b, j):
                pe.wait_ge(S["outT_copied"], HP * b + j + 1)
                if j < 2:
                    pe.wait_ge(S["att_done"], HP * b)
                else:
                    pe.wait_ge(S["att_done"], HP * b + j - 1)
                for c in range(C):
                    last = te.transpose(TR[j % 2][:, c * P:(c + 1) * P], att_T[:, j % 2, c * P:(c + 1) * P], ident[:])
                last.then_inc(S["tr_done"], 1)

            def step(b, q, first, last):
                work = {0: [], 1: [0, 1], 2: [2, 3], 3: [4, 5], 4: [6, 7], 5: []}
                for j in range(HP):
                    if not last:
                        for w in work[j]:
                            if w < C:
                                features(b + 1, w)
                            else:
                                gates(b + 1, w - C)
                    if j:
                        transpose_out(b, j - 1)
                    if j == 5 and not last:
                        means(b + 1)
                        transpose_v(b + 1)
                    attend(b, q, j, last)
                transpose_out(b, HP - 1)

            program(pe, step, before)


def kernel(x, adj, L0_gnn_W, L0_gnn_b, L0_gnn_w_src, L0_gnn_w_dst, L0_gnn_H_w, L0_gnn_H_b):
    import numpy as np
    import concourse.bacc as bacc
    from concourse.bass_utils import run_bass_kernel_spmd

    x, adj, W = np.asarray(x), np.asarray(adj), np.asarray(L0_gnn_W)
    H, D, E = W.shape
    arrays = {
        "x": x,
        "xT": x.transpose(0, 2, 1),
        "adjT": adj.transpose(0, 2, 1),
        "W": W.transpose(1, 0, 2).reshape(D, H * E),
        "HwT": np.asarray(L0_gnn_H_w).T,
        "w_src": np.asarray(L0_gnn_w_src).reshape(H, E),
        "w_dst": np.asarray(L0_gnn_w_dst).reshape(H, E),
        "bias": np.asarray(L0_gnn_b),
        "H_b": np.asarray(L0_gnn_H_b),
    }
    arrays = {f"in_{k}": np.ascontiguousarray(a) for k, a in arrays.items()}
    nc = bacc.Bacc("TRN2", target_bir_lowering=False, num_devices=1)
    args = [nc.dram_tensor(k, a.shape, mybir.dt.from_np(a.dtype), kind="ExternalInput").ap() for k, a in arrays.items()]
    out = nc.dram_tensor("out", x.shape, mybir.dt.from_np(x.dtype), kind="ExternalOutput").ap()
    gat_layernorm(nc, *args, out)
    r = run_bass_kernel_spmd(nc, [arrays], core_ids=[0])
    return r.results[0]["out"]
```

```python
import concourse.bass as bass
from concourse import mybir
from contextlib import ExitStack

F32 = mybir.dt.float32
F32R = mybir.dt.float32r
BF16 = mybir.dt.bfloat16
U8 = mybir.dt.uint8
ALU = mybir.AluOpType
ACT = mybir.ActivationFunctionType
AX = mybir.AxisListType
RMAX = bass.bass_isa.ReduceOp.max

P = 128
ALPHA = 0.2
EPS = 1e-5
TINY = 1.2e-38


def gat_layernorm(nc, x, xT, adjT, W, HwT, w_src, w_dst, bias, H_b, out):
    B, N, D = x.shape
    H, E = w_src.shape
    C = N // P
    KD = D // P
    HP = H // 2
    VW = 64
    SLOTS = 16
    NPART = 3
    assert N == 512 and H * E == D and B % 2 == 0

    ctx = ExitStack()
    with ctx:
        def sb(name, shape, dt=F32):
            return ctx.enter_context(nc.sbuf_tensor(name, shape, dt))

        def pb(name):
            return ctx.enter_context(nc.psum_tensor(name, [P, 512], F32))

        def sem(name):
            return ctx.enter_context(nc.semaphore(name))

        xT_in = sb("xT_in", [P, KD, N])
        xT_hi = sb("xT_hi", [P, KD, N], F32R)
        xT_lo = sb("xT_lo", [P, KD, N], F32R)
        x_in = sb("x_in", [P, C, D])
        adj_in = sb("adj_in", [P, 2, C, N], U8)
        w_hi = sb("w_hi", [P, KD, 2 * D], F32R)
        w_lo = sb("w_lo", [P, KD, 2 * D], F32R)
        src_row = sb("src_row", [P, D])
        dst_row = sb("dst_row", [P, D])
        bias_row = sb("bias_row", [P, H, E])
        gate_bias_in = sb("gate_bias_in", [P, D])
        gate_bias = sb("gate_bias", [P, D], F32R)
        gate_bias_sel = sb("gate_bias_sel", [P, P], F32R)
        ident = sb("ident", [P, P])
        ident_bf = sb("ident_bf", [P, P], BF16)
        head_sel = sb("head_sel", [P, H, P], BF16)
        mean_w = sb("mean_w", [P, P])
        half = sb("half", [P, C])
        minus1 = sb("minus1", [P, 1])
        plus1 = sb("plus1", [P, 1])
        h_sb = sb("h_sb", [P, C, D])
        hb_sum = sb("hb_sum", [P, 2, D])
        th = sb("th", [P, C, D])
        prod = sb("prod", [P, 2, C, D])
        sd = sb("sd", [P, 2, C, H])
        d_max_c = sb("d_max_c", [P, H])
        d_max = sb("d_max", [P, H])
        d_rel = sb("d_rel", [P, C, H])
        s_rel = sb("s_rel", [P, C, H])
        s_exp = sb("s_exp", [P, C, H])
        v = sb("v", [P, C, H])
        v_rest = sb("v_rest", [P, C, H])
        v_parts = sb("v_parts", [P, C, P], BF16)
        v_T = sb("v_T", [P, 2, N], BF16)
        u = sb("u", [P, 2, C, H])
        vals = sb("vals", [P, 2, C, H, VW])
        hb_mean = sb("hb_mean", [P, 2, D])
        gate_tanh = sb("gate_tanh", [P, C, D])
        gate = sb("gate", [P, 2, C, D])
        ew = sb("ew", [P, SLOTS, N])
        att_T = sb("att_T", [P, 2, N])
        den = sb("den", [P, C, 2])
        rden = sb("rden", [P, C, 2])
        alone = sb("alone", [P, C])
        att = sb("att", [P, 2, C, D])
        x_plus1 = sb("x_plus1", [P, C, D])
        x_times4 = sb("x_times4", [P, C, D])
        ex = sb("ex", [P, C, D])
        y = sb("y", [P, C, D])
        stats = sb("stats", [P, C, 6])
        mv = sb("mv", [P, C, 2])
        var = sb("var", [P, C])
        neg_mean = sb("neg_mean", [P, C])
        rstd = sb("rstd", [P, C])
        shift = sb("shift", [P, C])
        w_in = ew[:, 0:5, :].rearrange("p s n -> p (s n)")[:, 0:2 * KD * D].rearrange("p (k n) -> p k n", k=KD)

        HG = [pb("hg0"), pb("hg1")]
        VB = [pb("vb0"), pb("vb1"), pb("vb2")]
        OUT = pb("out_T")
        TR = [pb("tr0"), pb("tr1")]
        vtp = HG[1][:, 0:N // 2].bitcast(BF16)

        names = """ld_w ld_rows ld_xT ld_x ld_adj0 ld_adj1 st_y
            consts pool_setup dve_setup act_setup
            xhi_done xlo_done h_done th_done hcopy_done g_done gate_done hb_done hb_sum_done hm_done hm_copied
            prod_done scores d_max_done exps_done vtp_done vT_done vals_done
            vb_ready ew_ready ew_free outT_copied tr_done den_done att_done
            alone_done att1_done x_forms_done gate1_done elu_exp_done elu_done mixed moments rstd_done y_done""".split()
        S = {n: sem(n) for n in names}
        ld_adj = [S["ld_adj0"], S["ld_adj1"]]
        NSC = 9
        NMO = 2 * C + 2

        x_v = x.rearrange("b (c p) d -> b p c d", p=P)
        xT_v = xT.rearrange("b (k p) n -> b p k n", p=P)
        adj_v = adjT.rearrange("b (c p) n -> b p c n", p=P)
        out_v = out.rearrange("b (c p) d -> b p c d", p=P)

        block = ctx.enter_context(nc.Block())

        def program(eng, step, before=None, after=None):
            if before:
                before()
            step(0, 0, True, False)
            with eng.Fori(0, (B - 2) // 2) as i:
                step(2 * i + 1, 1, False, False)
                step(2 * i + 2, 0, False, False)
            step(B - 1, (B - 1) % 2, False, True)
            if after:
                after()

        @block.sync
        def _(sp):
            def before():
                sp.sem_inc(S["st_y"], 16)
                sp.dma_start(w_in[:, :, 0:D], W.rearrange("(k p) n -> p k n", p=P)).then_inc(S["ld_w"], 16)
                sp.dma_start(w_in[:, :, D:2 * D], HwT.rearrange("(k p) n -> p k n", p=P)).then_inc(S["ld_w"], 16)
                sp.dma_start(xT_in[:], xT_v[0]).then_inc(S["ld_xT"], 16)
                row = lambda a: a.rearrange("h e -> (h e)").rearrange("(o n) -> o n", o=1).broadcast_to([P, D])
                sp.dma_start(src_row[:], row(w_src)).then_inc(S["ld_rows"], 16)
                sp.dma_start(dst_row[:], row(w_dst)).then_inc(S["ld_rows"], 16)
                for hh in range(H):
                    sp.dma_start(bias_row[:, hh, :], bias.rearrange("(o n) -> o n", o=1).broadcast_to([P, E])).then_inc(S["ld_rows"], 16)
                sp.wait_ge(S["pool_setup"], 1)
                for r in (0, 32):
                    sp.dma_start(gate_bias_in[r:r + 1, :], H_b.rearrange("(o n) -> o n", o=1)).then_inc(S["ld_rows"], 16)
                sp.dma_start(adj_in[:, 0], adj_v[0]).then_inc(ld_adj[0], 16)

            def step(b, q, first, last):
                if not last:
                    sp.wait_ge(S["xhi_done"], b + 1)
                    sp.wait_ge(S["xlo_done"], b + 1)
                    sp.dma_start(xT_in[:], xT_v[b + 1]).then_inc(S["ld_xT"], 16)
                if not first:
                    sp.wait_ge(S["x_forms_done"], 2 * b)
                    sp.wait_ge(S["alone_done"], b + 1)
                sp.dma_start(x_in[:], x_v[b]).then_inc(S["ld_x"], 16)
                if not last:
                    sp.dma_start(adj_in[:, 1 - q], adj_v[b + 1]).then_inc(ld_adj[1 - q], 16)

            program(sp, step, before, lambda: sp.wait_ge(S["st_y"], 16 * B + 16))

        @block.gpsimd
        def _(pool):
            g = nc.gpsimd

            def before():
                g.sem_inc(S["mixed"], 3)
                g.memset(gate_bias_in[:], 0.0).then_inc(S["pool_setup"], 1)
                g.memset(ident[:], 0.0).then_inc(S["pool_setup"], 1)
                g.memset(ident_bf[:], 0.0).then_inc(S["pool_setup"], 1)
                g.memset(head_sel[:], 0.0).then_inc(S["pool_setup"], 1)
                g.memset(mean_w[:], 1.0 / N).then_inc(S["pool_setup"], 1)
                g.memset(half[:], -0.5).then_inc(S["pool_setup"], 1)
                g.memset(minus1[:], -1.0).then_inc(S["pool_setup"], 1)
                g.memset(plus1[:], 1.0).then_inc(S["pool_setup"], 1)
                pool.wait_ge(S["pool_setup"], 8)
                for m in (ident, ident_bf):
                    g.affine_select(out=m[:], in_=m[:], compare_op=ALU.not_equal, fill=1.0, base=0,
                                    pattern=[[-1, P]], channel_multiplier=1).then_inc(S["pool_setup"], 1)
                for k in range(NPART):
                    g.affine_select(out=head_sel[:], in_=head_sel[:], compare_op=ALU.not_equal, fill=1.0,
                                    base=-H * k, pattern=[[-1, H], [0, P]],
                                    channel_multiplier=1).then_inc(S["pool_setup"], 1)
                    pool.wait_ge(S["pool_setup"], 11 + k)
                pool.wait_ge(S["ld_w"], 32)
                pool.wait_ge(S["act_setup"], 1)
                g.tensor_tensor(w_lo[:], w_in, w_hi[:].bitcast(F32), ALU.subtract).then_inc(S["pool_setup"], 1)
                pool.wait_ge(S["ld_rows"], 16 * (4 + H))
                g.tensor_scalar(bias_row[:], bias_row[:], 1.0, 1.0, ALU.mult, ALU.add).then_inc(S["pool_setup"], 1)
                pool.wait_ge(S["pool_setup"], 15)
                prepare(0, 0, True)

            def prepare(b, q, first):
                pool.wait_ge(S["xhi_done"], b + 1)
                pool.wait_ge(S["g_done"], C * b)
                g.tensor_tensor(xT_lo[:], xT_in[:], xT_hi[:].bitcast(F32), ALU.subtract).then_inc(S["xlo_done"], 1)
                for c in range(C):
                    pool.wait_ge(S["th_done"], C * b + c + 1)
                    for k, row in ((0, src_row), (1, dst_row)):
                        g.tensor_tensor(prod[:, k, c], th[:, c], row[:], ALU.mult).then_inc(S["prod_done"], 1)
                    if c == C - 2 and not first:
                        subtract_x(b - 2)
                pool.wait_ge(S["hcopy_done"], C * b + C)
                g.tensor_tensor(h_sb[:], h_sb[:], bias_row[:].rearrange("p h e -> p (h e)").unsqueeze(1).broadcast_to([P, C, D]),
                                ALU.add).then_inc(S["hb_done"], 1)
                pool.wait_ge(S["hb_done"], b + 1)
                pool.wait_ge(S["hm_done"], b)
                pool.wait_ge(S["scores"], NSC * b + 2)
                g.tensor_tensor(hb_sum[:], h_sb[:, 0:2], h_sb[:, 2:4], ALU.add).then_inc(S["hb_sum_done"], 1)
                g.partition_all_reduce(d_max[:], d_max_c[:], P, RMAX).then_inc(S["d_max_done"], 1)
                if not first:
                    mix(b - 2, q)
                pool.wait_ge(S["exps_done"], 3 * b + 1)
                for c in range(C):
                    o = vals[:, q, c]
                    g.tensor_tensor(o[:, :, 0:E], h_sb[:, c].rearrange("p (h e) -> p h e", e=E),
                                    o[:, :, E:E + 1].broadcast_to([P, H, E]), ALU.mult).then_inc(S["vals_done"], 1)

            def subtract_x(b):
                pool.wait_ge(S["elu_done"], b + 1)
                pool.wait_ge(S["x_forms_done"], 2 * b + 2)
                g.tensor_tensor(ex[:], ex[:], x_plus1[:], ALU.subtract).then_inc(S["mixed"], 1)

            def mix(b, q):
                pool.wait_ge(S["gate1_done"], b + 1)
                pool.wait_ge(S["mixed"], 3 * b + 4)
                g.tensor_tensor(ex[:], gate[:, q], ex[:], ALU.mult).then_inc(S["mixed"], 1)
                pool.wait_ge(S["mixed"], 3 * b + 5)
                pool.wait_ge(S["st_y"], 16 * b + 16)
                g.tensor_tensor(y[:], x_times4[:], ex[:], ALU.add).then_inc(S["mixed"], 1)

            def scale(b):
                pool.wait_ge(S["moments"], NMO * b + NMO)
                g.tensor_tensor(rstd[:], var[:], half[:], ALU.pow).then_inc(S["rstd_done"], 1)
                pool.wait_ge(S["rstd_done"], 2 * b + 1)
                g.tensor_tensor(shift[:], neg_mean[:], rstd[:], ALU.mult).then_inc(S["rstd_done"], 1)

            def step(b, q, first, last):
                if not last:
                    prepare(b + 1, 1 - q, first)
                elif not first:
                    subtract_x(b - 1)
                    mix(b - 1, 1 - q)
                if not first:
                    scale(b - 1)

            def after():
                subtract_x(B - 1)
                mix(B - 1, (B - 1) % 2)
                scale(B - 1)

            program(pool, step, before, after)

        @block.scalar
        def _(act):
            a = nc.scalar

            def before():
                act.wait_ge(S["ld_w"], 32)
                a.activation(w_hi[:], w_in, ACT.Copy).then_inc(S["act_setup"], 1)
                split(0)
                for c in range(C):
                    features(0, c)
                for c in range(C):
                    gates(0, 0, c, True)
                act.wait_ge(S["pool_setup"], 15)
                exps(0, 0)
                copy_mean(0, 0)
                copy_vT(0, 0)

            def split(b):
                act.wait_ge(S["ld_xT"], 16 * b + 16)
                act.wait_ge(S["g_done"], C * b)
                a.activation(xT_hi[:], xT_in[:], ACT.Copy).then_inc(S["xhi_done"], 1)

            def features(b, c):
                act.wait_ge(S["h_done"], C * b + c + 1)
                act.wait_ge(S["prod_done"], 2 * C * b)
                a.activation(th[:, c], HG[c % 2][:, 0:D], ACT.Tanh).then_inc(S["th_done"], 1)
                act.wait_ge(S["vals_done"], C * b)
                a.activation(h_sb[:, c], HG[c % 2][:, 0:D], ACT.Copy).then_inc(S["hcopy_done"], 1)

            def gates(b, q, c, first):
                act.wait_ge(S["g_done"], C * b + c + 1)
                if not first:
                    act.wait_ge(S["gate1_done"], b)
                a.activation(gate_tanh[:, c], HG[c % 2][:, 0:D], ACT.Tanh, scale=0.5).then_inc(S["gate_done"], 1)

            def exps(b, q):
                act.wait_ge(S["scores"], NSC * b + 3)
                a.activation(vals[:, q, :, :, E], d_rel[:], ACT.Exp, scale=ALPHA).then_inc(S["exps_done"], 1)
                a.activation(u[:, q], d_rel[:], ACT.Exp, scale=1 - ALPHA).then_inc(S["exps_done"], 1)
                act.wait_ge(S["scores"], NSC * b + 5)
                a.activation(v[:], s_exp[:], ACT.Exp).then_inc(S["exps_done"], 1)

            def copy_mean(b, q):
                act.wait_ge(S["hm_done"], b + 1)
                a.activation(hb_mean[:, q], HG[0][:, 0:D], ACT.Copy).then_inc(S["hm_copied"], 1)

            def copy_vT(b, q):
                act.wait_ge(S["vtp_done"], b + 1)
                a.activation(v_T[:, q], vtp, ACT.Copy).then_inc(S["vT_done"], 1)

            def copy_out(b, j):
                act.wait_ge(S["ew_free"], SLOTS + 4 * H * b + 8 * j + 8)
                if j > 1 or not isinstance(b, int) or b:
                    act.wait_ge(S["tr_done"], HP * b + j - 1)
                a.activation(att_T[:, j % 2], OUT[:], ACT.Copy).then_inc(S["outT_copied"], 1)

            def x_forms(b):
                act.wait_ge(S["ld_x"], 16 * b + 16)
                act.wait_ge(S["mixed"], 3 * b + 3)
                a.activation(x_plus1[:], x_in[:], ACT.Identity, bias=plus1[:, 0:1]).then_inc(S["x_forms_done"], 1)
                a.activation(x_times4[:], x_in[:], ACT.Copy, scale=4.0).then_inc(S["x_forms_done"], 1)

            def gate_plus1(b, q):
                act.wait_ge(S["gate_done"], C * b + C)
                a.activation(gate[:, q], gate_tanh[:], ACT.Identity, bias=plus1[:, 0:1]).then_inc(S["gate1_done"], 1)

            def elu_exp(b, q):
                act.wait_ge(S["att1_done"], C * b + C)
                a.activation(ex[:], att[:, q], ACT.Exp, bias=minus1[:, 0:1]).then_inc(S["elu_exp_done"], 1)

            def normalise(b):
                act.wait_ge(S["rstd_done"], 2 * b + 2)
                for c in range(C):
                    a.activation(y[:, c], y[:, c], ACT.Identity, bias=shift[:, c:c + 1],
                                 scale=rstd[:, c:c + 1]).then_inc(S["y_done"], 1)
                act.wait_ge(S["y_done"], C * b + C)
                act.dma_start(out_v[b], y[:]).then_inc(S["st_y"], 16)

            def step(b, q, first, last):
                if not last:
                    split(b + 1)
                if not first:
                    x_forms(b - 1)
                gate_plus1(b, q)
                copy_out(b, 0)
                if not first:
                    elu_exp(b - 1, 1 - q)
                if not last:
                    for c in range(3):
                        features(b + 1, c)
                copy_out(b, 1)
                if not last:
                    features(b + 1, 3)
                    gates(b + 1, 1 - q, 0, first)
                copy_out(b, 2)
                if not last:
                    gates(b + 1, 1 - q, 1, first)
                    gates(b + 1, 1 - q, 2, first)
                copy_out(b, 3)
                if not last:
                    exps(b + 1, 1 - q)
                    gates(b + 1, 1 - q, 3, first)
                    copy_mean(b + 1, 1 - q)
                copy_out(b, 4)
                if not last:
                    copy_vT(b + 1, 1 - q)
                copy_out(b, 5)
                if not first:
                    normalise(b - 1)

            def after():
                x_forms(B - 1)
                elu_exp(B - 1, (B - 1) % 2)
                normalise(B - 1)

            program(act, step, before, after)

        @block.vector
        def _(dve):
            ve = nc.vector

            def before():
                ve.memset(vals[:, :, :, :, :], 0.0).then_inc(S["dve_setup"], 1)
                ve.memset(v_parts[:], 0.0).then_inc(S["dve_setup"], 1)
                ve.memset(gate_bias_sel[:].bitcast(F32), 0.0).then_inc(S["dve_setup"], 1)
                dve.wait_ge(S["dve_setup"], 3)
                for r in (0, 32):
                    ve.memset(gate_bias_sel[r:r + 1, :].bitcast(F32), 1.0).then_inc(S["dve_setup"], 1)
                dve.wait_ge(S["ld_rows"], 16 * (4 + H))
                ve.tensor_copy(gate_bias[:], gate_bias_in[:]).then_inc(S["dve_setup"], 1)
                dve.wait_ge(S["dve_setup"], 6)
                ve.tensor_tensor(gate_bias[32:33, :], gate_bias_in[32:33, :], gate_bias[32:33, :].bitcast(F32),
                                 ALU.subtract).then_inc(S["dve_setup"], 1)
                dve.wait_ge(S["dve_setup"], 7)
                scores_sd(0)
                for f in scores_rel(0) + split_v(0):
                    f()

            def sc(b, k):
                dve.wait_ge(S["scores"], NSC * b + k)

            def scores_sd(b):
                dve.wait_ge(S["prod_done"], 2 * C * (b + 1))
                ve.tensor_reduce(sd[:].rearrange("p k c h -> p (k c h)"), prod[:].rearrange("p k c (h e) -> p (k c h) e", e=E),
                                 AX.X, ALU.add).then_inc(S["scores"], 1)
                sc(b, 1)
                ve.tensor_reduce(d_max_c[:], sd[:, 1].rearrange("p c h -> p h c"), AX.X, ALU.max).then_inc(S["scores"], 1)

            def scores_rel(b):
                m = d_max[:].unsqueeze(1).broadcast_to([P, C, H])

                def relative():
                    dve.wait_ge(S["d_max_done"], b + 1)
                    ve.tensor_tensor(d_rel[:], sd[:, 1], m, ALU.subtract).then_inc(S["scores"], 1)
                    ve.tensor_tensor(s_rel[:], sd[:, 0], m, ALU.add).then_inc(S["scores"], 1)

                def exponent():
                    sc(b, 4)
                    ve.tensor_scalar(s_exp[:], s_rel[:], ALPHA - 1, 0.0, ALU.mult, ALU.min).then_inc(S["scores"], 1)

                return [relative, exponent]

            def split_v(b):

                def high():
                    dve.wait_ge(S["exps_done"], 3 * b + 3)
                    dve.wait_ge(S["vtp_done"], b)
                    ve.tensor_copy(v_parts[:, :, 0:H], v[:]).then_inc(S["scores"], 1)

                def rest():
                    sc(b, 6)
                    ve.tensor_tensor(v_rest[:], v[:], v_parts[:, :, 0:H], ALU.subtract).then_inc(S["scores"], 1)

                def middle():
                    sc(b, 7)
                    ve.tensor_copy(v_parts[:, :, H:2 * H], v_rest[:]).then_inc(S["scores"], 1)

                def low():
                    sc(b, 8)
                    ve.tensor_tensor(v_parts[:, :, 2 * H:3 * H], v_rest[:], v_parts[:, :, H:2 * H],
                                     ALU.subtract).then_inc(S["scores"], 1)

                return [high, rest, middle, low]

            def edges(b, q, h, between=()):
                dve.wait_ge(S["vb_ready"], H * b + h + 1)
                for c in range(C):
                    for f in between[c - 1:c] if c else ():
                        f()
                    t = 8 * (h // 2) + 4 * (h % 2) + c
                    dve.wait_ge(S["ew_free"], 4 * H * b + 8 * (h // 2) + 2 * c + h % 2 + 1)
                    ve.scalar_tensor_tensor(out=ew[:, t % SLOTS, :], in0=VB[h % 3][:], scalar=u[:, q, c, h:h + 1],
                                            in1=adj_in[:, q, c, :], op0=ALU.max, op1=ALU.mult).then_inc(S["ew_ready"], 1)

            def attended(b, q, j):
                t = TR[j % 2][:].rearrange("p (c k w) -> p c k w", c=C, k=2)

                def denominators():
                    dve.wait_ge(S["tr_done"], HP * b + j + 1)
                    if j == 0:
                        ve.tensor_scalar(alone[:], t[:, :, 0, E], 0.0, None, ALU.is_equal).then_inc(S["alone_done"], 1)
                    ve.tensor_scalar(den[:], t[:, :, :, E], TINY, None, ALU.max).then_inc(S["den_done"], 1)

                def inverses():
                    dve.wait_ge(S["den_done"], 2 * (HP * b + j) + 1)
                    ve.reciprocal(rden[:], den[:]).then_inc(S["den_done"], 1)

                def quotients():
                    dve.wait_ge(S["den_done"], 2 * (HP * b + j) + 2)
                    o = att[:, q].rearrange("p c (h e) -> p c h e", e=E)[:, :, 2 * j:2 * j + 2, :]
                    ve.tensor_tensor(o, t[:, :, :, 0:E], rden[:].unsqueeze(3).broadcast_to([P, C, 2, E]),
                                     ALU.mult).then_inc(S["att_done"], 1)

                return [denominators, inverses, quotients]

            def add_means(b, q):
                dve.wait_ge(S["att_done"], HP * b + HP)
                dve.wait_ge(S["hm_copied"], b + 1)
                dve.wait_ge(S["alone_done"], b + 1)
                for c in range(C):
                    ve.scalar_tensor_tensor(out=att[:, q, c], in0=hb_mean[:, q], scalar=alone[:, c:c + 1],
                                            in1=att[:, q, c], op0=ALU.mult, op1=ALU.add).then_inc(S["att1_done"], 1)

            def elu(b, q):
                dve.wait_ge(S["elu_exp_done"], b + 1)
                dve.wait_ge(S["att1_done"], C * b + C)
                ve.scalar_tensor_tensor(out=ex[:], in0=ex[:], scalar=1.0, in1=att[:, q], op0=ALU.min,
                                        op1=ALU.max).then_inc(S["elu_done"], 1)

            def statistics(b):
                dve.wait_ge(S["mixed"], 3 * b + 6)
                for c in range(C):
                    ve.bn_stats(stats[:, c], y[:, c]).then_inc(S["moments"], 1)

            def statistics_done(b):
                dve.wait_ge(S["moments"], NMO * b + C)

            def aggregate(b):
                for c in range(C):
                    ve.bn_aggr(mv[:, c], stats[:, c]).then_inc(S["moments"], 1)
                dve.wait_ge(S["moments"], NMO * b + 2 * C)
                ve.tensor_scalar(var[:], mv[:, :, 1], 4 * EPS, None, ALU.add).then_inc(S["moments"], 1)
                ve.tensor_scalar(neg_mean[:], mv[:, :, 0], -1.0, None, ALU.mult).then_inc(S["moments"], 1)

            def step(b, q, first, last):
                dve.wait_ge(ld_adj[q], 8 * (b - q) + 16)
                dve.wait_ge(S["exps_done"], 3 * b + 3)
                for j in range(HP):
                    steps = scores_rel(b + 1) if j == 4 and not last else split_v(b + 1)[:3] if j == 5 and not last else []
                    edges(b, q, 2 * j, steps)
                    if j == 1 and not first:
                        elu(b - 1, 1 - q)
                    if j == 3 and not last:
                        scores_sd(b + 1)
                    if j == 5 and not last:
                        split_v(b + 1)[3]()
                    if j == 5 and not first:
                        statistics(b - 1)
                        statistics_done(b - 1)
                    if j:
                        edges(b, q, 2 * j + 1, attended(b, q, j - 1))
                    elif not first:
                        edges(b, q, 1, attended(b - 1, 1 - q, HP - 1))
                        add_means(b - 1, 1 - q)
                    else:
                        edges(b, q, 1)
                    if j == 5 and not first:
                        aggregate(b - 1)

            def after():
                q = (B - 1) % 2
                for f in attended(B - 1, q, HP - 1):
                    f()
                add_means(B - 1, q)
                elu(B - 1, q)
                statistics(B - 1)
                statistics_done(B - 1)
                aggregate(B - 1)

            program(dve, step, before, after)

        @block.tensor
        def _(pe):
            te = nc.tensor

            def before():
                te.sem_inc(S["ew_free"], SLOTS)
                pe.wait_ge(S["pool_setup"], 15)
                pe.wait_ge(S["dve_setup"], 7)
                for c in range(C):
                    features(0, c)
                for c in range(C):
                    gates(0, c)
                means(0)
                transpose_v(0)
                broadcast_v(0, 0, 0)
                broadcast_v(0, 0, 1)

            def products(bank, c, col, extra):
                o = bank[:, 0:D]
                n = slice(c * P, (c + 1) * P)
                mms = []
                for k in range(KD):
                    mms += [(xT_hi[:, k, n], w_hi[:, k, col:col + D]), (xT_hi[:, k, n], w_lo[:, k, col:col + D])]
                for k in range(KD):
                    mms.append((xT_lo[:, k, n], w_hi[:, k, col:col + D]))
                mms += extra
                for i, (l, r) in enumerate(mms):
                    last = te.matmul(o, l, r, start=(i == 0), stop=(i == len(mms) - 1))
                return last

            def features(b, c):
                if c == 0:
                    pe.wait_ge(S["xhi_done"], b + 1)
                    pe.wait_ge(S["xlo_done"], b + 1)
                if c == 0:
                    pe.wait_ge(S["hm_copied"], b)
                elif c == 1:
                    pe.wait_ge(S["vT_done"], b)
                else:
                    pe.wait_ge(S["hcopy_done"], C * b + c - 1)
                products(HG[c % 2], c, 0, []).then_inc(S["h_done"], 1)

            def gates(b, c):
                if c < 2:
                    pe.wait_ge(S["hcopy_done"], C * b + c + 3)
                else:
                    pe.wait_ge(S["gate_done"], C * b + c - 1)
                products(HG[c % 2], c, D, [(gate_bias_sel[:], gate_bias[:])]).then_inc(S["g_done"], 1)

            def means(b):
                pe.wait_ge(S["hb_sum_done"], b + 1)
                pe.wait_ge(S["gate_done"], C * b + 3)
                for k in range(2):
                    last = te.matmul(HG[0][:, 0:D], mean_w[:], hb_sum[:, k], start=(k == 0), stop=(k == 1))
                last.then_inc(S["hm_done"], 1)

            def transpose_v(b):
                pe.wait_ge(S["scores"], NSC * b + NSC)
                pe.wait_ge(S["gate_done"], C * b + C)
                for c in range(C):
                    last = te.transpose(vtp[:, c * P:(c + 1) * P], v_parts[:, c], ident_bf[:])
                last.then_inc(S["vtp_done"], 1)

            def broadcast_v(b, q, h):
                if h == 0:
                    pe.wait_ge(S["vT_done"], b + 1)
                if h > 2 or not isinstance(b, int) or b:
                    pe.wait_ge(S["ew_ready"], 4 * H * b + 4 * (h - 2))
                te.matmul(VB[h % 3][:], head_sel[:, h], v_T[:, q], start=True, stop=True).then_inc(S["vb_ready"], 1)

            def broadcast_ahead(b, q, h, last):
                if h < H:
                    broadcast_v(b, q, h)
                elif not last:
                    broadcast_v(b + 1, 1 - q, h - H)

            def attend(b, q, j, last):
                if j or not isinstance(b, int) or b:
                    pe.wait_ge(S["outT_copied"], HP * b + j)
                if j == 0:
                    pe.wait_ge(S["vals_done"], C * b + C)
                for c in range(C):
                    for k in range(2):
                        h = 2 * j + k
                        t = 8 * j + 4 * k + c
                        if (c, k) == ((0, 1) if j < HP - 1 else (3, 0)):
                            broadcast_ahead(b, q, 2 * j + 3, last)
                        if j == HP - 1 and (c, k) == (1, 1):
                            broadcast_ahead(b, q, 2 * j + 2, last)
                        pe.wait_ge(S["ew_ready"], 4 * H * b + t + 1)
                        te.matmul(OUT[VW * k:VW * k + VW, :], vals[:, q, c, h, :], ew[:, t % SLOTS, :],
                                  start=(c == 0), stop=(c == C - 1)).then_inc(S["ew_free"], 1)

            def transpose_out(b, j):
                pe.wait_ge(S["outT_copied"], HP * b + j + 1)
                if j > 1 or not isinstance(b, int) or b:
                    pe.wait_ge(S["att_done"], HP * b + j - 1)
                for c in range(C):
                    last = te.transpose(TR[j % 2][:, c * P:(c + 1) * P], att_T[:, j % 2, c * P:(c + 1) * P], ident[:])
                last.then_inc(S["tr_done"], 1)

            groups = {1: [(features, 0), (features, 1), (features, 2)], 2: [(features, 3), (gates, 0)],
                      3: [(gates, 1), (gates, 2)], 4: [(gates, 3)]}

            def step(b, q, first, last):
                for j in range(HP):
                    if j < HP - 1:
                        broadcast_ahead(b, q, 2 * j + 2, last)
                    work = [] if last else groups.get(j, [])
                    for f, c in work[:1]:
                        f(b + 1, c)
                    if j:
                        transpose_out(b, j - 1)
                    elif not first:
                        transpose_out(b - 1, HP - 1)
                    for f, c in work[1:]:
                        f(b + 1, c)
                    if j == HP - 2 and not last:
                        means(b + 1)
                    if j < HP - 1:
                        attend(b, q, j, last)
                    else:
                        if not last:
                            transpose_v(b + 1)
                        attend(b, q, j, last)

            def after():
                transpose_out(B - 1, HP - 1)

            program(pe, step, before, after)


def kernel(x, adj, L0_gnn_W, L0_gnn_b, L0_gnn_w_src, L0_gnn_w_dst, L0_gnn_H_w, L0_gnn_H_b):
    import numpy as np
    import concourse.bacc as bacc
    from concourse.bass_utils import run_bass_kernel_spmd

    x, adj, W = np.asarray(x), np.asarray(adj), np.asarray(L0_gnn_W)
    H, D, E = W.shape
    arrays = {
        "x": x,
        "xT": x.transpose(0, 2, 1),
        "adjT": adj.transpose(0, 2, 1),
        "W": W.transpose(1, 0, 2).reshape(D, H * E),
        "HwT": np.asarray(L0_gnn_H_w).T,
        "w_src": np.asarray(L0_gnn_w_src).reshape(H, E),
        "w_dst": np.asarray(L0_gnn_w_dst).reshape(H, E),
        "bias": np.asarray(L0_gnn_b),
        "H_b": np.asarray(L0_gnn_H_b),
    }
    arrays = {f"in_{k}": np.ascontiguousarray(a) for k, a in arrays.items()}
    nc = bacc.Bacc("TRN2", target_bir_lowering=False, num_devices=1)
    args = [nc.dram_tensor(k, a.shape, mybir.dt.from_np(a.dtype), kind="ExternalInput").ap() for k, a in arrays.items()]
    out = nc.dram_tensor("out", x.shape, mybir.dt.from_np(x.dtype), kind="ExternalOutput").ap()
    gat_layernorm(nc, *args, out)
    r = run_bass_kernel_spmd(nc, [arrays], core_ids=[0])
    return r.results[0]["out"]
```

```python
import concourse.bass as bass
from concourse import mybir
from contextlib import ExitStack

F32 = mybir.dt.float32
F32R = mybir.dt.float32r
BF16 = mybir.dt.bfloat16
U8 = mybir.dt.uint8
ALU = mybir.AluOpType
ACT = mybir.ActivationFunctionType
AX = mybir.AxisListType
RMAX = bass.bass_isa.ReduceOp.max

P = 128
ALPHA = 0.2
EPS = 1e-5
TINY = 1.2e-38


def gat_layernorm(nc, x, xT, adjT, W, HwT, w_cols, bias, H_b, out):
    B, N, D = x.shape
    E = bias.shape[0]
    H = D // E
    C = N // P
    KD = D // P
    HP = H // 2
    VW = 64
    SLOTS = 16
    NPART = 3
    assert N == 512 and H * E == D and B % 2 == 0

    ctx = ExitStack()
    with ctx:
        def sb(name, shape, dt=F32):
            return ctx.enter_context(nc.sbuf_tensor(name, shape, dt))

        def pb(name):
            return ctx.enter_context(nc.psum_tensor(name, [P, 512], F32))

        def sem(name):
            return ctx.enter_context(nc.semaphore(name))

        xT_in = sb("xT_in", [P, KD, N])
        xT_hi = sb("xT_hi", [P, KD, N], F32R)
        xT_lo = sb("xT_lo", [P, KD, N], F32R)
        x_in = sb("x_in", [P, C, D])
        adj_in = sb("adj_in", [P, 2, C, N], U8)
        w_hi = sb("w_hi", [P, KD, 2 * D], F32R)
        w_lo = sb("w_lo", [P, KD, 2 * D], F32R)
        score_cols = sb("score_cols", [P, KD, 2])
        score_w = sb("score_w", [P, KD, 2, H])
        bias_row = sb("bias_row", [P, H, E])
        gate_bias_in = sb("gate_bias_in", [P, D])
        gate_bias = sb("gate_bias", [P, D], F32R)
        gate_bias_sel = sb("gate_bias_sel", [P, P], F32R)
        ident = sb("ident", [P, P])
        ident_bf = sb("ident_bf", [P, P], BF16)
        head_sel = sb("head_sel", [P, H, P], BF16)
        mean_w = sb("mean_w", [P, P])
        half = sb("half", [P, C])
        minus1 = sb("minus1", [P, 1])
        plus1 = sb("plus1", [P, 1])
        h_sb = sb("h_sb", [P, C, D])
        hb_sum = sb("hb_sum", [P, 2, D])
        th_T = sb("th_T", [P, KD, N])
        sd_ckh = sb("sd", [P, C * 2 * H])
        sd = sd_ckh[:].rearrange("p (c k h) -> p k c h", c=C, k=2)
        d_max_c = sb("d_max_c", [P, H])
        d_max = sb("d_max", [P, H])
        d_rel = sb("d_rel", [P, C, H])
        s_rel = sb("s_rel", [P, C, H])
        s_exp = sb("s_exp", [P, C, H])
        v = sb("v", [P, C, H])
        v_rest = sb("v_rest", [P, C, H])
        v_parts = sb("v_parts", [P, C, P], BF16)
        v_T = sb("v_T", [P, 2, N], BF16)
        u = sb("u", [P, 2, C, H])
        vals = sb("vals", [P, 2, C, H, VW])
        hb_mean = sb("hb_mean", [P, 2, D])
        gate_tanh = sb("gate_tanh", [P, C, D])
        gate = sb("gate", [P, 2, C, D])
        ew = sb("ew", [P, SLOTS, N])
        att_T = sb("att_T", [P, 2, N])
        den = sb("den", [P, C, 2])
        rden = sb("rden", [P, C, 2])
        alone = sb("alone", [P, C])
        att = sb("att", [P, 2, C, D])
        x_plus1 = sb("x_plus1", [P, C, D])
        x_times4 = sb("x_times4", [P, C, D])
        ex = sb("ex", [P, C, D])
        y = sb("y", [P, C, D])
        stats = sb("stats", [P, C, 6])
        mv = sb("mv", [P, C, 2])
        var = sb("var", [P, C])
        neg_mean = sb("neg_mean", [P, C])
        rstd = sb("rstd", [P, C])
        shift = sb("shift", [P, C])
        w_in = ew[:, 0:5, :].rearrange("p s n -> p (s n)")[:, 0:2 * KD * D].rearrange("p (k n) -> p k n", k=KD)

        HG = [pb("hg0"), pb("hg1")]
        VB = [pb("vb0"), pb("vb1"), pb("vb2")]
        OUT = pb("out_T")
        TR = [pb("tr0"), pb("tr1")]
        vtp = HG[1][:, 0:N // 2].bitcast(BF16)

        names = """st_last ld_w ld_wg ld_cols ld_rows ld_xT ld_x ld_adj0 ld_adj1 st_y
            pool_setup dve_setup
            w_hi_done w_lo_done xhi_done xlo_done h_done hT_done th_done sd_done sd_copied hcopy_done g_done gate_done hb_done hb_sum_done hm_done hm_copied
            scores d_max_done exps_done vtp_done vT_done vals_done
            vb_ready ew_ready ew_free outT_copied tr_done den_done att_done
            alone_done att1_done x_forms_done gate1_done elu_exp_done elu_done mixed moments rstd_done y_done last_mixed last_y_done""".split()
        S = {n: sem(n) for n in names}
        ld_adj = [S["ld_adj0"], S["ld_adj1"]]
        NSC = 8
        NMO = 2 * C + 2

        x_v = x.rearrange("b (c p) d -> b p c d", p=P)
        xT_v = xT.rearrange("b (k p) n -> b p k n", p=P)
        adj_v = adjT.rearrange("b (c p) n -> b p c n", p=P)
        out_v = out.rearrange("b (c p) d -> b p c d", p=P)

        block = ctx.enter_context(nc.Block())

        def program(eng, step, before=None, after=None):
            if before:
                before()
            step(0, 0, True, False)
            with eng.Fori(0, (B - 2) // 2) as i:
                step(2 * i + 1, 1, False, False)
                step(2 * i + 2, 0, False, False)
            step(B - 1, (B - 1) % 2, False, True)
            if after:
                after()

        @block.sync
        def _(sp):
            def before():
                sp.sem_inc(S["st_y"], 16)
                sp.dma_start(w_in[:, :, 0:D], W.rearrange("(k p) n -> p k n", p=P)).then_inc(S["ld_w"], 16)
                sp.dma_start(xT_in[:], xT_v[0]).then_inc(S["ld_xT"], 16)
                sp.dma_start(w_in[:, :, D:2 * D], HwT.rearrange("(k p) n -> p k n", p=P)).then_inc(S["ld_wg"], 16)
                sp.dma_start(score_cols[:], w_cols).then_inc(S["ld_cols"], 16)
                sp.dma_start(bias_row[:], bias.rearrange("(o q n) -> o q n", o=1, q=1).broadcast_to([P, H, E])).then_inc(S["ld_rows"], 16)
                sp.wait_ge(S["pool_setup"], 1)
                for r in (0, 32):
                    sp.dma_start(gate_bias_in[r:r + 1, :], H_b.rearrange("(o n) -> o n", o=1)).then_inc(S["ld_rows"], 16)
                sp.dma_start(adj_in[:, 0], adj_v[0]).then_inc(ld_adj[0], 16)

            def step(b, q, first, last):
                if not last:
                    sp.wait_ge(S["xhi_done"], b + 1)
                    sp.wait_ge(S["xlo_done"], b + 1)
                    sp.dma_start(xT_in[:], xT_v[b + 1]).then_inc(S["ld_xT"], 16)
                if not first:
                    sp.wait_ge(S["x_forms_done"], 2 * b)
                    sp.wait_ge(S["alone_done"], b + 1)
                sp.dma_start(x_in[:], x_v[b]).then_inc(S["ld_x"], 16)
                if not last:
                    sp.dma_start(adj_in[:, 1 - q], adj_v[b + 1]).then_inc(ld_adj[1 - q], 16)

            def after():
                sp.wait_ge(S["last_y_done"], 2)
                sp.dma_start(out_v[B - 1][:, 2:C], y[:, 2:C]).then_inc(S["st_last"], 16)
                sp.wait_ge(S["st_y"], 16 * B + 16)
                sp.wait_ge(S["st_last"], 16)

            program(sp, step, before, after)

        @block.gpsimd
        def _(pool):
            g = nc.gpsimd

            def before():
                g.sem_inc(S["mixed"], 3)
                g.memset(gate_bias_in[:], 0.0).then_inc(S["pool_setup"], 1)
                g.memset(ident[:], 0.0).then_inc(S["pool_setup"], 1)
                g.memset(ident_bf[:], 0.0).then_inc(S["pool_setup"], 1)
                g.memset(head_sel[:], 0.0).then_inc(S["pool_setup"], 1)
                g.memset(mean_w[:], 1.0 / N).then_inc(S["pool_setup"], 1)
                g.memset(half[:], -0.5).then_inc(S["pool_setup"], 1)
                g.memset(minus1[:], -1.0).then_inc(S["pool_setup"], 1)
                g.memset(plus1[:], 1.0).then_inc(S["pool_setup"], 1)
                pool.wait_ge(S["pool_setup"], 8)
                for m in (ident, ident_bf):
                    g.affine_select(out=m[:], in_=m[:], compare_op=ALU.not_equal, fill=1.0, base=0,
                                    pattern=[[-1, P]], channel_multiplier=1).then_inc(S["pool_setup"], 1)
                for k in range(NPART):
                    g.affine_select(out=head_sel[:], in_=head_sel[:], compare_op=ALU.not_equal, fill=1.0,
                                    base=-H * k, pattern=[[-1, H], [0, P]],
                                    channel_multiplier=1).then_inc(S["pool_setup"], 1)
                    pool.wait_ge(S["pool_setup"], 11 + k)
                pool.wait_ge(S["ld_cols"], 16)
                g.tensor_scalar(score_w[:], score_cols[:].unsqueeze(3).broadcast_to([P, KD, 2, H]), 1.0, 0.0,
                                ALU.mult, ALU.add).then_inc(S["pool_setup"], 1)
                pool.wait_ge(S["pool_setup"], 14)
                g.affine_select(out=score_w[:], in_=score_w[:], compare_op=ALU.is_ge, fill=0.0, base=0,
                                pattern=[[P, KD], [0, 2], [-E, H]], channel_multiplier=1).then_inc(S["pool_setup"], 1)
                pool.wait_ge(S["pool_setup"], 15)
                g.affine_select(out=score_w[:], in_=score_w[:], compare_op=ALU.is_ge, fill=0.0, base=E - 1,
                                pattern=[[-P, KD], [0, 2], [E, H]], channel_multiplier=-1).then_inc(S["pool_setup"], 1)
                pool.wait_ge(S["ld_rows"], 16 * 3)
                g.tensor_scalar(bias_row[:], bias_row[:], 1.0, 1.0, ALU.mult, ALU.add).then_inc(S["pool_setup"], 1)
                pool.wait_ge(S["pool_setup"], 17)
                prepare(0, 0, True, start=True)

            def prepare(b, q, first, start=False):
                if not start:
                    pool.wait_ge(S["xhi_done"], b + 1)
                    pool.wait_ge(S["g_done"], C * b)
                    g.tensor_tensor(xT_lo[:], xT_in[:], xT_hi[:].bitcast(F32), ALU.subtract).then_inc(S["xlo_done"], 1)
                if not first:
                    subtract_x(b - 2)
                pool.wait_ge(S["hT_done"], KD * b + KD)
                g.tensor_tensor(h_sb[:], h_sb[:], bias_row[:].rearrange("p h e -> p (h e)").unsqueeze(1).broadcast_to([P, C, D]),
                                ALU.add).then_inc(S["hb_done"], 1)
                pool.wait_ge(S["hb_done"], b + 1)
                pool.wait_ge(S["hm_done"], b)
                pool.wait_ge(S["scores"], NSC * b + 1)
                g.tensor_tensor(hb_sum[:], h_sb[:, 0:2], h_sb[:, 2:4], ALU.add).then_inc(S["hb_sum_done"], 1)
                g.partition_all_reduce(d_max[:], d_max_c[:], P, RMAX).then_inc(S["d_max_done"], 1)
                pool.wait_ge(S["hb_sum_done"], 2 * b + 1)
                g.tensor_tensor(hb_sum[:, 0], hb_sum[:, 0], hb_sum[:, 1], ALU.add).then_inc(S["hb_sum_done"], 1)
                if not first:
                    mix(b - 2, q)
                pool.wait_ge(S["exps_done"], 3 * b + 1)
                for c in range(C):
                    o = vals[:, q, c]
                    g.tensor_tensor(o[:, :, 0:E], h_sb[:, c].rearrange("p (h e) -> p h e", e=E),
                                    o[:, :, E:E + 1].broadcast_to([P, H, E]), ALU.mult).then_inc(S["vals_done"], 1)

            def subtract_x(b):
                pool.wait_ge(S["elu_done"], b + 1)
                pool.wait_ge(S["x_forms_done"], 2 * b + 2)
                g.tensor_tensor(ex[:], ex[:], x_plus1[:], ALU.subtract).then_inc(S["mixed"], 1)

            def mix(b, q):
                pool.wait_ge(S["gate1_done"], b + 1)
                pool.wait_ge(S["mixed"], 3 * b + 4)
                g.tensor_tensor(ex[:], gate[:, q], ex[:], ALU.mult).then_inc(S["mixed"], 1)
                pool.wait_ge(S["mixed"], 3 * b + 5)
                pool.wait_ge(S["st_y"], 16 * b + 16)
                g.tensor_tensor(y[:], x_times4[:], ex[:], ALU.add).then_inc(S["mixed"], 1)

            def scale(b):
                pool.wait_ge(S["moments"], NMO * b + NMO)
                g.tensor_tensor(rstd[:], var[:], half[:], ALU.pow).then_inc(S["rstd_done"], 1)
                pool.wait_ge(S["rstd_done"], 2 * b + 1)
                g.tensor_tensor(shift[:], neg_mean[:], rstd[:], ALU.mult).then_inc(S["rstd_done"], 1)

            def step(b, q, first, last):
                if not last:
                    prepare(b + 1, 1 - q, first)
                elif not first:
                    subtract_x(b - 1)
                    mix(b - 1, 1 - q)
                if not first:
                    scale(b - 1)

            def after():
                scale(B - 1)

            program(pool, step, before, after)

        @block.scalar
        def _(act):
            a = nc.scalar

            def before():
                act.wait_ge(S["ld_w"], 16)
                a.activation(w_hi[:, :, 0:D], w_in[:, :, 0:D], ACT.Copy).then_inc(S["w_hi_done"], 1)
                split(0)
                act.wait_ge(S["ld_wg"], 16)
                a.activation(w_hi[:, :, D:2 * D], w_in[:, :, D:2 * D], ACT.Copy).then_inc(S["w_hi_done"], 1)
                for c in range(C):
                    features(0, c)
                for k in range(KD):
                    tanh_T(0, k)
                copy_sd(0)
                for c in range(C):
                    gates(0, 0, c, True)
                act.wait_ge(S["pool_setup"], 17)
                act.wait_ge(S["dve_setup"], 7)
                exps(0, 0)
                copy_mean(0, 0)
                copy_vT(0, 0)

            def split(b):
                act.wait_ge(S["ld_xT"], 16 * b + 16)
                act.wait_ge(S["g_done"], C * b)
                a.activation(xT_hi[:], xT_in[:], ACT.Copy).then_inc(S["xhi_done"], 1)

            def features(b, c):
                act.wait_ge(S["h_done"], C * b + c + 1)
                act.wait_ge(S["vals_done"], C * b)
                a.activation(h_sb[:, c], HG[c % 2][:, 0:D], ACT.Copy).then_inc(S["hcopy_done"], 1)

            def tanh_T(b, k):
                act.wait_ge(S["hT_done"], KD * b + k + 1)
                act.wait_ge(S["sd_done"], b)
                a.activation(th_T[:, k], HG[k % 2][:], ACT.Tanh).then_inc(S["th_done"], 1)

            def copy_sd(b):
                act.wait_ge(S["sd_done"], b + 1)
                act.wait_ge(S["scores"], NSC * b)
                a.activation(sd_ckh[:], HG[1][:, 0:2 * H * C], ACT.Copy).then_inc(S["sd_copied"], 1)

            def gates(b, q, c, first):
                act.wait_ge(S["g_done"], C * b + c + 1)
                if not first:
                    act.wait_ge(S["gate1_done"], b)
                a.activation(gate_tanh[:, c], HG[c % 2][:, 0:D], ACT.Tanh, scale=0.5).then_inc(S["gate_done"], 1)

            def exps(b, q):
                act.wait_ge(S["scores"], NSC * b + 2)
                a.activation(vals[:, q, :, :, E], d_rel[:], ACT.Exp, scale=ALPHA).then_inc(S["exps_done"], 1)
                a.activation(u[:, q], d_rel[:], ACT.Exp, scale=1 - ALPHA).then_inc(S["exps_done"], 1)
                act.wait_ge(S["scores"], NSC * b + 4)
                a.activation(v[:], s_exp[:], ACT.Exp).then_inc(S["exps_done"], 1)

            def copy_mean(b, q):
                act.wait_ge(S["hm_done"], b + 1)
                a.activation(hb_mean[:, q], HG[0][:, 0:D], ACT.Copy).then_inc(S["hm_copied"], 1)

            def copy_vT(b, q):
                act.wait_ge(S["vtp_done"], b + 1)
                a.activation(v_T[:, q], vtp, ACT.Copy).then_inc(S["vT_done"], 1)

            def copy_out(b, j):
                act.wait_ge(S["ew_free"], SLOTS + 4 * H * b + 8 * j + 8)
                if j > 1 or not isinstance(b, int) or b:
                    act.wait_ge(S["tr_done"], HP * b + j - 1)
                a.activation(att_T[:, j % 2], OUT[:], ACT.Copy).then_inc(S["outT_copied"], 1)

            def x_forms(b):
                act.wait_ge(S["ld_x"], 16 * b + 16)
                act.wait_ge(S["mixed"], 3 * b + 3)
                a.activation(x_plus1[:], x_in[:], ACT.Identity, bias=plus1[:, 0:1]).then_inc(S["x_forms_done"], 1)
                a.activation(x_times4[:], x_in[:], ACT.Copy, scale=4.0).then_inc(S["x_forms_done"], 1)

            def gate_plus1(b, q):
                act.wait_ge(S["gate_done"], C * b + C)
                a.activation(gate[:, q], gate_tanh[:], ACT.Identity, bias=plus1[:, 0:1]).then_inc(S["gate1_done"], 1)

            def elu_exp(b, q):
                act.wait_ge(S["att1_done"], C * b + C)
                a.activation(ex[:], att[:, q], ACT.Exp, bias=minus1[:, 0:1]).then_inc(S["elu_exp_done"], 1)

            def normalise(b):
                act.wait_ge(S["rstd_done"], 2 * b + 2)
                for c in range(C):
                    a.activation(y[:, c], y[:, c], ACT.Identity, bias=shift[:, c:c + 1],
                                 scale=rstd[:, c:c + 1]).then_inc(S["y_done"], 1)
                act.wait_ge(S["y_done"], C * b + C)
                act.dma_start(out_v[b], y[:]).then_inc(S["st_y"], 16)

            def step(b, q, first, last):
                if not last:
                    split(b + 1)
                if not first:
                    x_forms(b - 1)
                gate_plus1(b, q)
                copy_out(b, 0)
                if not first:
                    elu_exp(b - 1, 1 - q)
                if not last:
                    for c in range(3):
                        features(b + 1, c)
                copy_out(b, 1)
                if not last:
                    features(b + 1, 3)
                    for k in range(KD):
                        tanh_T(b + 1, k)
                copy_out(b, 2)
                if not last:
                    copy_sd(b + 1)
                    gates(b + 1, 1 - q, 0, first)
                copy_out(b, 3)
                if not last:
                    gates(b + 1, 1 - q, 1, first)
                    exps(b + 1, 1 - q)
                    gates(b + 1, 1 - q, 2, first)
                copy_out(b, 4)
                if not last:
                    gates(b + 1, 1 - q, 3, first)
                    copy_mean(b + 1, 1 - q)
                    copy_vT(b + 1, 1 - q)
                if not first:
                    normalise(b - 1)
                copy_out(b, 5)
                if last:
                    x_forms(b)

            def after():
                act.wait_ge(S["att1_done"], C * B)
                for c in range(C):
                    a.activation(ex[:, c], att[:, (B - 1) % 2, c], ACT.Exp, bias=minus1[:, 0:1]).then_inc(S["elu_exp_done"], 1)
                act.wait_ge(S["rstd_done"], 2 * B)
                for c in range(2):
                    a.activation(y[:, c], y[:, c], ACT.Identity, bias=shift[:, c:c + 1],
                                 scale=rstd[:, c:c + 1]).then_inc(S["y_done"], 1)
                act.wait_ge(S["y_done"], C * (B - 1) + 2)
                act.dma_start(out_v[B - 1][:, 0:2], y[:, 0:2]).then_inc(S["st_y"], 16)

            program(act, step, before, after)

        @block.vector
        def _(dve):
            ve = nc.vector

            def before():
                ve.memset(v_parts[:], 0.0).then_inc(S["dve_setup"], 1)
                ve.memset(gate_bias_sel[:].bitcast(F32), 0.0).then_inc(S["dve_setup"], 1)
                dve.wait_ge(S["dve_setup"], 2)
                for r in (0, 32):
                    ve.memset(gate_bias_sel[r:r + 1, :].bitcast(F32), 1.0).then_inc(S["dve_setup"], 1)
                for k in range(2):
                    dve.wait_ge(S[("ld_w", "ld_wg")[k]], 16)
                    dve.wait_ge(S["w_hi_done"], k + 1)
                    n = slice(k * D, (k + 1) * D)
                    ve.tensor_tensor(w_lo[:, :, n], w_in[:, :, n], w_hi[:, :, n].bitcast(F32),
                                     ALU.subtract).then_inc(S["w_lo_done"], 1)
                    if k == 0:
                        dve.wait_ge(S["xhi_done"], 1)
                        ve.tensor_tensor(xT_lo[:], xT_in[:], xT_hi[:].bitcast(F32), ALU.subtract).then_inc(S["xlo_done"], 1)
                dve.wait_ge(S["ld_rows"], 16 * 3)
                ve.tensor_copy(gate_bias[:], gate_bias_in[:]).then_inc(S["dve_setup"], 1)
                dve.wait_ge(S["dve_setup"], 5)
                ve.tensor_tensor(gate_bias[32:33, :], gate_bias_in[32:33, :], gate_bias[32:33, :].bitcast(F32),
                                 ALU.subtract).then_inc(S["dve_setup"], 1)
                ve.memset(vals[:], 0.0).then_inc(S["dve_setup"], 1)
                dve.wait_ge(S["dve_setup"], 7)
                scores_max(0)
                for f in scores_rel(0) + split_v(0):
                    f()

            def sc(b, k):
                dve.wait_ge(S["scores"], NSC * b + k)

            def scores_max(b):
                dve.wait_ge(S["sd_copied"], b + 1)
                ve.tensor_reduce(d_max_c[:], sd[:, 1].rearrange("p c h -> p h c"), AX.X, ALU.max).then_inc(S["scores"], 1)

            def scores_rel(b):
                m = d_max[:].unsqueeze(1).broadcast_to([P, C, H])

                def relative():
                    dve.wait_ge(S["d_max_done"], b + 1)
                    ve.tensor_tensor(d_rel[:], sd[:, 1], m, ALU.subtract).then_inc(S["scores"], 1)
                    ve.tensor_tensor(s_rel[:], sd[:, 0], m, ALU.add).then_inc(S["scores"], 1)

                def exponent():
                    sc(b, 3)
                    ve.tensor_scalar(s_exp[:], s_rel[:], ALPHA - 1, 0.0, ALU.mult, ALU.min).then_inc(S["scores"], 1)

                return [relative, exponent]

            def split_v(b):

                def high():
                    dve.wait_ge(S["exps_done"], 3 * b + 3)
                    dve.wait_ge(S["vtp_done"], b)
                    ve.tensor_copy(v_parts[:, :, 0:H], v[:]).then_inc(S["scores"], 1)

                def rest():
                    sc(b, 5)
                    ve.tensor_tensor(v_rest[:], v[:], v_parts[:, :, 0:H], ALU.subtract).then_inc(S["scores"], 1)

                def middle():
                    sc(b, 6)
                    ve.tensor_copy(v_parts[:, :, H:2 * H], v_rest[:]).then_inc(S["scores"], 1)

                def low():
                    sc(b, 7)
                    ve.tensor_tensor(v_parts[:, :, 2 * H:3 * H], v_rest[:], v_parts[:, :, H:2 * H],
                                     ALU.subtract).then_inc(S["scores"], 1)

                return [high, rest, middle, low]

            def edges(b, q, h, between=()):
                dve.wait_ge(S["vb_ready"], H * b + h + 1)
                for c in range(C):
                    for f in between[c - 1:c] if c else ():
                        f()
                    t = C * h + c
                    dve.wait_ge(S["ew_free"], 4 * H * b + t + 1)
                    ve.scalar_tensor_tensor(out=ew[:, t % SLOTS, :], in0=VB[h % 3][:], scalar=u[:, q, c, h:h + 1],
                                            in1=adj_in[:, q, c, :], op0=ALU.max, op1=ALU.mult).then_inc(S["ew_ready"], 1)

            def attended(b, q, j):
                t = TR[j % 2][:].rearrange("p (c k w) -> p c k w", c=C, k=2)

                def denominators():
                    dve.wait_ge(S["tr_done"], HP * b + j + 1)
                    if j == 0:
                        ve.tensor_scalar(alone[:], t[:, :, 0, E], 0.0, None, ALU.is_equal).then_inc(S["alone_done"], 1)
                    ve.tensor_scalar(den[:], t[:, :, :, E], TINY, None, ALU.max).then_inc(S["den_done"], 1)

                def inverses():
                    dve.wait_ge(S["den_done"], 2 * (HP * b + j) + 1)
                    ve.reciprocal(rden[:], den[:]).then_inc(S["den_done"], 1)

                def quotients():
                    dve.wait_ge(S["den_done"], 2 * (HP * b + j) + 2)
                    o = att[:, q].rearrange("p c (h e) -> p c h e", e=E)[:, :, 2 * j:2 * j + 2, :]
                    ve.tensor_tensor(o, t[:, :, :, 0:E], rden[:].unsqueeze(3).broadcast_to([P, C, 2, E]),
                                     ALU.mult).then_inc(S["att_done"], 1)

                return [denominators, inverses, quotients]

            def add_means(b, q):
                dve.wait_ge(S["att_done"], HP * b + HP)
                dve.wait_ge(S["hm_copied"], b + 1)
                dve.wait_ge(S["alone_done"], b + 1)
                for c in range(C):
                    ve.scalar_tensor_tensor(out=att[:, q, c], in0=hb_mean[:, q], scalar=alone[:, c:c + 1],
                                            in1=att[:, q, c], op0=ALU.mult, op1=ALU.add).then_inc(S["att1_done"], 1)

            def elu(b, q):
                dve.wait_ge(S["elu_exp_done"], b + 1)
                ve.scalar_tensor_tensor(out=ex[:], in0=ex[:], scalar=1.0, in1=att[:, q], op0=ALU.min,
                                        op1=ALU.max).then_inc(S["elu_done"], 1)

            def statistics(b):
                dve.wait_ge(S["mixed"], 3 * b + 6)
                for c in range(C):
                    ve.bn_stats(stats[:, c], y[:, c]).then_inc(S["moments"], 1)

            def statistics_done(b):
                dve.wait_ge(S["moments"], NMO * b + C)

            def aggregate(b):
                for c in range(C):
                    ve.bn_aggr(mv[:, c], stats[:, c]).then_inc(S["moments"], 1)
                dve.wait_ge(S["moments"], NMO * b + 2 * C)
                ve.tensor_scalar(var[:], mv[:, :, 1], 4 * EPS, None, ALU.add).then_inc(S["moments"], 1)
                ve.tensor_scalar(neg_mean[:], mv[:, :, 0], -1.0, None, ALU.mult).then_inc(S["moments"], 1)

            def step(b, q, first, last):
                dve.wait_ge(ld_adj[q], 8 * (b - q) + 16)
                dve.wait_ge(S["exps_done"], 3 * b + 3)
                for j in range(HP):
                    steps = scores_rel(b + 1) if j == 4 and not last else split_v(b + 1)[:3] if j == 5 and not last else []
                    edges(b, q, 2 * j, steps)
                    if j == 1 and not first:
                        elu(b - 1, 1 - q)
                    if j == 3 and not last:
                        scores_max(b + 1)
                    if j == 5 and not last:
                        split_v(b + 1)[3]()
                    if j == 5 and not first:
                        aggregate(b - 1)
                    if j:
                        edges(b, q, 2 * j + 1, attended(b, q, j - 1))
                    elif not first:
                        edges(b, q, 1, attended(b - 1, 1 - q, HP - 1))
                        add_means(b - 1, 1 - q)
                    else:
                        edges(b, q, 1)
                    if j == 4 and not first:
                        statistics(b - 1)
                        statistics_done(b - 1)

            def after():
                q = (B - 1) % 2
                for f in attended(B - 1, q, HP - 1):
                    f()
                add_means(B - 1, q)
                for c in range(C):
                    dve.wait_ge(S["elu_exp_done"], B + c)
                    ve.scalar_tensor_tensor(out=ex[:, c], in0=ex[:, c], scalar=1.0, in1=att[:, q, c], op0=ALU.min,
                                            op1=ALU.max).then_inc(S["last_mixed"], 1)
                dve.wait_ge(S["x_forms_done"], 2 * B)
                dve.wait_ge(S["gate1_done"], B)
                dve.wait_ge(S["st_y"], 16 * B)
                for i, (o, l, r, op) in enumerate(((ex, ex, x_plus1, ALU.subtract), (ex, gate[:, q], ex, ALU.mult),
                                                   (y, x_times4, ex, ALU.add))):
                    for c in range(C):
                        dve.wait_ge(S["last_mixed"], C * i + c + 1)
                        ve.tensor_tensor(o[:, c], l[:, c], r[:, c], op).then_inc(S["last_mixed"], 1)
                dve.wait_ge(S["last_mixed"], 4 * C)
                for c in range(C):
                    ve.bn_stats(stats[:, c], y[:, c]).then_inc(S["moments"], 1)
                statistics_done(B - 1)
                aggregate(B - 1)
                dve.wait_ge(S["rstd_done"], 2 * B)
                for c in range(2, C):
                    ve.tensor_scalar(y[:, c], y[:, c], rstd[:, c:c + 1], shift[:, c:c + 1],
                                     ALU.mult, ALU.add).then_inc(S["last_y_done"], 1)

            program(dve, step, before, after)

        @block.tensor
        def _(pe):
            te = nc.tensor

            def before():
                te.sem_inc(S["ew_free"], SLOTS)
                pe.wait_ge(S["w_lo_done"], 1)
                for c in range(C):
                    features(0, c)
                pe.wait_ge(S["pool_setup"], 17)
                for k in range(KD):
                    transpose_h(0, k)
                score_sums(0)
                pe.wait_ge(S["w_lo_done"], 2)
                pe.wait_ge(S["dve_setup"], 6)
                for c in range(C):
                    gates(0, c)
                means(0)
                transpose_v(0)
                broadcast_v(0, 0, 0)
                broadcast_v(0, 0, 1)

            def products(bank, c, col, extra):
                o = bank[:, 0:D]
                n = slice(c * P, (c + 1) * P)
                mms = []
                for k in range(KD):
                    mms += [(xT_hi[:, k, n], w_hi[:, k, col:col + D]), (xT_hi[:, k, n], w_lo[:, k, col:col + D])]
                for k in range(KD):
                    mms.append((xT_lo[:, k, n], w_hi[:, k, col:col + D]))
                mms += extra
                for i, (l, r) in enumerate(mms):
                    last = te.matmul(o, l, r, start=(i == 0), stop=(i == len(mms) - 1))
                return last

            def features(b, c):
                if c == 0:
                    pe.wait_ge(S["xhi_done"], b + 1)
                    pe.wait_ge(S["xlo_done"], b + 1)
                if c == 0:
                    pe.wait_ge(S["hm_copied"], b)
                elif c == 1:
                    pe.wait_ge(S["vT_done"], b)
                else:
                    pe.wait_ge(S["hcopy_done"], C * b + c - 1)
                products(HG[c % 2], c, 0, []).then_inc(S["h_done"], 1)

            def transpose_h(b, k):
                if k == 0:
                    pe.wait_ge(S["hcopy_done"], C * b + C)
                elif k == 2:
                    pe.wait_ge(S["th_done"], KD * b + 1)
                for c in range(C):
                    last = te.transpose(HG[k % 2][:, c * P:(c + 1) * P], h_sb[:, c, k * P:(k + 1) * P], ident[:])
                last.then_inc(S["hT_done"], 1)

            def score_sums(b):
                pe.wait_ge(S["th_done"], KD * b + KD)
                for c in range(C):
                    for k in range(KD):
                        last = te.matmul(HG[1][:, 2 * H * c:2 * H * (c + 1)], th_T[:, k, c * P:(c + 1) * P],
                                         score_w[:, k].rearrange("p s h -> p (s h)"), start=(k == 0), stop=(k == KD - 1))
                last.then_inc(S["sd_done"], 1)

            def gates(b, c):
                if c == 0:
                    pe.wait_ge(S["th_done"], KD * b + KD)
                elif c == 1:
                    pe.wait_ge(S["sd_copied"], b + 1)
                else:
                    pe.wait_ge(S["gate_done"], C * b + c - 1)
                products(HG[c % 2], c, D, [(gate_bias_sel[:], gate_bias[:])]).then_inc(S["g_done"], 1)

            def means(b):
                pe.wait_ge(S["hb_sum_done"], 2 * b + 2)
                pe.wait_ge(S["gate_done"], C * b + 3)
                te.matmul(HG[0][:, 0:D], mean_w[:], hb_sum[:, 0], start=True, stop=True).then_inc(S["hm_done"], 1)

            def transpose_v(b):
                pe.wait_ge(S["scores"], NSC * b + NSC)
                pe.wait_ge(S["gate_done"], C * b + C)
                for c in range(C):
                    last = te.transpose(vtp[:, c * P:(c + 1) * P], v_parts[:, c], ident_bf[:])
                last.then_inc(S["vtp_done"], 1)

            def broadcast_v(b, q, h):
                if h == 0:
                    pe.wait_ge(S["vT_done"], b + 1)
                if h > 2 or not isinstance(b, int) or b:
                    pe.wait_ge(S["ew_ready"], 4 * H * b + 4 * (h - 2))
                te.matmul(VB[h % 3][:], head_sel[:, h], v_T[:, q], start=True, stop=True).then_inc(S["vb_ready"], 1)

            def attend(b, q, j, last):
                if j or not isinstance(b, int) or b:
                    pe.wait_ge(S["outT_copied"], HP * b + j)
                if j == 0:
                    pe.wait_ge(S["vals_done"], C * b + C)
                for k in range(2):
                    for c in range(C):
                        h = 2 * j + k
                        t = C * h + c
                        if j == HP - 1 and (c, k) in ((3, 0), (2, 1)) and not last:
                            broadcast_v(b + 1, 1 - q, k)
                        pe.wait_ge(S["ew_ready"], 4 * H * b + t + 1)
                        te.matmul(OUT[VW * k:VW * k + VW, :], vals[:, q, c, h, :], ew[:, t % SLOTS, :],
                                  start=(c == 0), stop=(c == C - 1)).then_inc(S["ew_free"], 1)

            def transpose_out(b, j):
                pe.wait_ge(S["outT_copied"], HP * b + j + 1)
                if j > 1 or not isinstance(b, int) or b:
                    pe.wait_ge(S["att_done"], HP * b + j - 1)
                for c in range(C):
                    last = te.transpose(TR[j % 2][:, c * P:(c + 1) * P], att_T[:, j % 2, c * P:(c + 1) * P], ident[:])
                last.then_inc(S["tr_done"], 1)

            plan = [["back", "ahead"],
                    [(features, 0), "back", (features, 1), "ahead", (features, 2)],
                    [(features, 3), "back", (transpose_h, 0), "ahead", (transpose_h, 1), (transpose_h, 2)],
                    [(score_sums,), "back", "ahead", (gates, 0)],
                    [(gates, 1), "back", "ahead", (gates, 2)],
                    [(gates, 3), "back", (means,), (transpose_v,)]]

            def step(b, q, first, last):
                for j in range(HP):
                    if j < HP - 1:
                        broadcast_v(b, q, 2 * j + 2)
                    for item in plan[j]:
                        if item == "back":
                            if j:
                                transpose_out(b, j - 1)
                            elif not first:
                                transpose_out(b - 1, HP - 1)
                        elif item == "ahead":
                            broadcast_v(b, q, 2 * j + 3)
                        elif not last:
                            item[0](b + 1, *item[1:])
                    attend(b, q, j, last)

            def after():
                transpose_out(B - 1, HP - 1)

            program(pe, step, before, after)


def kernel(x, adj, L0_gnn_W, L0_gnn_b, L0_gnn_w_src, L0_gnn_w_dst, L0_gnn_H_w, L0_gnn_H_b):
    import numpy as np
    import concourse.bacc as bacc
    from concourse.bass_utils import run_bass_kernel_spmd

    x, adj, W = np.asarray(x), np.asarray(adj), np.asarray(L0_gnn_W)
    H, D, E = W.shape
    arrays = {
        "x": x,
        "xT": x.transpose(0, 2, 1),
        "adjT": adj.transpose(0, 2, 1),
        "W": W.transpose(1, 0, 2).reshape(D, H * E),
        "HwT": np.asarray(L0_gnn_H_w).T,
        "w_cols": np.stack([np.asarray(L0_gnn_w_src), np.asarray(L0_gnn_w_dst)]).reshape(2, D // P, P).transpose(2, 1, 0),
        "bias": np.asarray(L0_gnn_b),
        "H_b": np.asarray(L0_gnn_H_b),
    }
    arrays = {f"in_{k}": np.ascontiguousarray(a) for k, a in arrays.items()}
    nc = bacc.Bacc("TRN2", target_bir_lowering=False, num_devices=1)
    args = [nc.dram_tensor(k, a.shape, mybir.dt.from_np(a.dtype), kind="ExternalInput").ap() for k, a in arrays.items()]
    out = nc.dram_tensor("out", x.shape, mybir.dt.from_np(x.dtype), kind="ExternalOutput").ap()
    gat_layernorm(nc, *args, out)
    r = run_bass_kernel_spmd(nc, [arrays], core_ids=[0])
    return r.results[0]["out"]
```
